# Optimizing a Trainium2 kernel written in Bass

```python
import numpy as np
import jax
import jax.numpy as jnp

def _softmax(x, axis=-1):
    return jax.nn.softmax(x, axis=axis)

def _gelu(x):
    return jax.nn.gelu(x, approximate=True)

def _silu(x):
    return jax.nn.silu(x)

def _sigmoid(x):
    return jax.nn.sigmoid(x)

def _layernorm(x, axis=-1, eps=1e-05):
    m = jnp.mean(x, axis=axis, keepdims=True)
    v = jnp.var(x, axis=axis, keepdims=True)
    return (x - m) / jnp.sqrt(v + eps)

def _scatter_add(tgt, idx, src, axis=0):
    return tgt.at[idx].add(src)

def _segment_sum(src, seg, n):
    return jax.ops.segment_sum(src, seg, n)
kernel_name = 'mk_macaron_d1_jaxref_r8_d39879'

def setup_inputs(seed: int=0):
    np.random.seed(seed)
    _w = jnp.asarray

    def _L0_attn_setup():
        import jax, jax.numpy as jnp
        import numpy as np
        B, T, C, H = (2, 256, 128, 16)
        HD = C // H
        key = jax.random.key(seed)
        ks = jax.random.split(key, 9)
        s = 1.0 / np.sqrt(C)
        return {'x': jax.random.normal(ks[0], (B, T, C), dtype=jnp.float32), 'Wq': jax.random.normal(ks[1], (C, C), dtype=jnp.float32) * s, 'bq': jax.random.normal(ks[2], (C,), dtype=jnp.float32) * s, 'Wk': jax.random.normal(ks[3], (C, C), dtype=jnp.float32) * s, 'bk': jax.random.normal(ks[4], (C,), dtype=jnp.float32) * s, 'Wv': jax.random.normal(ks[5], (C, C), dtype=jnp.float32) * s, 'bv': jax.random.normal(ks[6], (C,), dtype=jnp.float32) * s, 'Wo': jax.random.normal(ks[7], (C, C), dtype=jnp.float32) * s, 'bo': jax.random.normal(ks[8], (C,), dtype=jnp.float32) * s}
    _L0_attn_in = _L0_attn_setup()

    def _L0_ffn_setup():
        import jax, jax.numpy as jnp
        import numpy as np
        DIM = 128
        DEPTH = 2
        HEADS = 8
        DIM_HEAD = 64
        WINDOW = 64
        INNER = HEADS * DIM_HEAD
        HID = int(DIM * 4 * 2 / 3)
        B, N = (2, 1024)
        QK_SCALE = 8.0

        def shift_token(t):
            t1, t2 = jnp.split(t, 2, axis=-1)
            t2 = jnp.pad(t2, ((0, 0), (1, 0), (0, 0)))[:, :-1]
            return jnp.concatenate([t1, t2], axis=-1)

        def l2norm(t):
            return t / jnp.clip(jnp.linalg.norm(t, axis=-1, keepdims=True), 1e-12)

        def rotate_half(x):
            x1, x2 = jnp.split(x, 2, axis=-1)
            return jnp.concatenate([-x2, x1], axis=-1)

        def rotary_xpos(q, k):
            n = q.shape[-2]
            half_idx = jnp.arange(0, DIM_HEAD, 2, dtype=jnp.float32)
            inv_freq = 1.0 / 10000.0 ** (half_idx / DIM_HEAD)
            t = jnp.arange(n, dtype=jnp.float32)
            freqs = t[:, None] * inv_freq[None, :]
            freqs = jnp.concatenate([freqs, freqs], axis=-1)
            base = (half_idx + 0.4 * DIM_HEAD) / (1.4 * DIM_HEAD)
            power = (t - n // 2) / float(WINDOW // 2)
            scale = base[None, :] ** power[:, None]
            scale = jnp.concatenate([scale, scale], axis=-1)
            cos, sin = (jnp.cos(freqs), jnp.sin(freqs))
            q = q * cos * scale + rotate_half(q) * sin * scale
            k = k * cos / scale + rotate_half(k) * sin / scale
            return (q, k)

        def local_attention(q, k, v):
            b, h, n, d = q.shape
            w = n // WINDOW
            bq = q.reshape(b, h, w, WINDOW, d) * QK_SCALE
            bk = k.reshape(b, h, w, WINDOW, d)
            bv = v.reshape(b, h, w, WINDOW, d)

            def look_around(t):
                p = jnp.pad(t, ((0, 0), (0, 0), (1, 0), (0, 0), (0, 0)))
                return jnp.concatenate([p[:, :, :w], p[:, :, 1:]], axis=3)
            bk, bv = (look_around(bk), look_around(bv))
            bt = jnp.arange(n).reshape(w, WINDOW)
            btp = jnp.pad(bt, ((1, 0), (0, 0)), constant_values=-1)
            btk = jnp.concatenate([btp[:w], btp[1:]], axis=1)
            sim = jnp.einsum('bhwid,bhwjd->bhwij', bq, bk)
            i = bt[:, :, None]
            j = btk[:, None, :]
            mask = (i < j) | (i > j + WINDOW) | (j == -1)
            sim = jnp.where(mask, -jnp.finfo(sim.dtype).max, sim)
            attn = jax.nn.softmax(sim, axis=-1)
            out = jnp.einsum('bhwij,bhwjd->bhwid', attn, bv)
            return out.reshape(b, h, n, d)

        def _layer(x, wqkv, qs, ksc, wo, lg, lb, w1, b1, w2, b2):
            b, n, _ = x.shape
            h = shift_token(x)
            qkv = h @ wqkv
            q, k, v = jnp.split(qkv, 3, axis=-1)
            to_heads = lambda t: t.reshape(b, n, HEADS, DIM_HEAD).transpose(0, 2, 1, 3)
            q, k, v = (to_heads(q), to_heads(k), to_heads(v))
            q = l2norm(q) * qs
            k = l2norm(k) * ksc
            q, k = rotary_xpos(q, k)
            o = local_attention(q, k, v)
            o = o.transpose(0, 2, 1, 3).reshape(b, n, INNER)
            x = x + o @ wo
            h = shift_token(x)
            mu = h.mean(-1, keepdims=True)
            var = h.var(-1, keepdims=True)
            h = (h - mu) / jnp.sqrt(var + 1e-05) * lg + lb
            h = h @ w1 + b1
            a, g = jnp.split(h, 2, axis=-1)
            h = a * jax.nn.gelu(g, approximate=False)
            x = x + h @ w2 + b2
            return x
        key = jax.random.key(seed)
        ks = jax.random.split(key, 6)
        return {'x': jax.random.normal(ks[0], (B, N, DIM), jnp.float32), 'wqkv': jax.random.normal(ks[1], (DEPTH, DIM, 3 * INNER), jnp.float32) * 0.02, 'q_scale': jnp.ones((DEPTH, DIM_HEAD), jnp.float32), 'k_scale': jnp.ones((DEPTH, DIM_HEAD), jnp.float32), 'wo': jax.random.normal(ks[2], (DEPTH, INNER, DIM), jnp.float32) * 0.02, 'ln_g': jnp.ones((DEPTH, DIM), jnp.float32), 'ln_b': jnp.zeros((DEPTH, DIM), jnp.float32), 'w1': jax.random.normal(ks[3], (DEPTH, DIM, 2 * HID), jnp.float32) * 0.02, 'b1': jnp.zeros((DEPTH, 2 * HID), jnp.float32), 'w2': jax.random.normal(ks[4], (DEPTH, HID, DIM), jnp.float32) * 0.02, 'b2': jnp.zeros((DEPTH, DIM), jnp.float32)}
    _L0_ffn_in = _L0_ffn_setup()
    _d = {'L0_attn_x': _L0_attn_in['x'], 'L0_attn_Wq': _L0_attn_in['Wq'], 'L0_attn_bq': _L0_attn_in['bq'], 'L0_attn_Wk': _L0_attn_in['Wk'], 'L0_attn_bk': _L0_attn_in['bk'], 'L0_attn_Wv': _L0_attn_in['Wv'], 'L0_attn_bv': _L0_attn_in['bv'], 'L0_attn_Wo': _L0_attn_in['Wo'], 'L0_attn_bo': _L0_attn_in['bo'], 'L0_ffn_wqkv': _L0_ffn_in['wqkv'], 'L0_ffn_q_scale': _L0_ffn_in['q_scale'], 'L0_ffn_k_scale': _L0_ffn_in['k_scale'], 'L0_ffn_wo': _L0_ffn_in['wo'], 'L0_ffn_ln_g': _L0_ffn_in['ln_g'], 'L0_ffn_ln_b': _L0_ffn_in['ln_b'], 'L0_ffn_w1': _L0_ffn_in['w1'], 'L0_ffn_b1': _L0_ffn_in['b1'], 'L0_ffn_w2': _L0_ffn_in['w2'], 'L0_ffn_b2': _L0_ffn_in['b2']}
    _x0 = _d['L0_attn_x']
    _d['L0_attn_x'] = jax.random.normal(jax.random.fold_in(jax.random.key(seed), 1), (16, 256, 128), dtype=_x0.dtype)
    del _x0
    return _d

def reference(L0_attn_x, L0_attn_Wq, L0_attn_bq, L0_attn_Wk, L0_attn_bk, L0_attn_Wv, L0_attn_bv, L0_attn_Wo, L0_attn_bo, L0_ffn_wqkv, L0_ffn_q_scale, L0_ffn_k_scale, L0_ffn_wo, L0_ffn_ln_g, L0_ffn_ln_b, L0_ffn_w1, L0_ffn_b1, L0_ffn_w2, L0_ffn_b2):

    def _L0_attn_ref(x, Wq, bq, Wk, bk, Wv, bv, Wo, bo):
        import jax, jax.numpy as jnp
        import numpy as np
        B, T, C, H = (2, 256, 128, 16)
        HD = C // H
        Bx, Tx, Cx = x.shape
        q = (x @ Wq + bq).reshape(Bx, Tx, H, HD).transpose(0, 2, 1, 3)
        k = (x @ Wk + bk).reshape(Bx, Tx, H, HD).transpose(0, 2, 1, 3)
        v = (x @ Wv + bv).reshape(Bx, Tx, H, HD).transpose(0, 2, 1, 3)
        scores = jnp.einsum('bhqd,bhkd->bhqk', q, k) / np.sqrt(HD).astype(np.float32)
        causal = jnp.tril(jnp.ones((Tx, Tx), dtype=bool))
        scores = jnp.where(causal, scores, -jnp.inf)
        weights = jax.nn.softmax(scores, axis=-1)
        out = jnp.einsum('bhqk,bhkd->bhqd', weights, v)
        out = out.transpose(0, 2, 1, 3).reshape(Bx, Tx, Cx)
        return out @ Wo + bo

    def _L0_ffn_ref(x, wqkv, q_scale, k_scale, wo, ln_g, ln_b, w1, b1, w2, b2):
        import jax, jax.numpy as jnp
        import numpy as np
        DIM = 128
        DEPTH = 2
        HEADS = 8
        DIM_HEAD = 64
        WINDOW = 64
        INNER = HEADS * DIM_HEAD
        HID = int(DIM * 4 * 2 / 3)
        B, N = (2, 1024)
        QK_SCALE = 8.0

        def shift_token(t):
            t1, t2 = jnp.split(t, 2, axis=-1)
            t2 = jnp.pad(t2, ((0, 0), (1, 0), (0, 0)))[:, :-1]
            return jnp.concatenate([t1, t2], axis=-1)

        def l2norm(t):
            return t / jnp.clip(jnp.linalg.norm(t, axis=-1, keepdims=True), 1e-12)

        def rotate_half(x):
            x1, x2 = jnp.split(x, 2, axis=-1)
            return jnp.concatenate([-x2, x1], axis=-1)

        def rotary_xpos(q, k):
            n = q.shape[-2]
            half_idx = jnp.arange(0, DIM_HEAD, 2, dtype=jnp.float32)
            inv_freq = 1.0 / 10000.0 ** (half_idx / DIM_HEAD)
            t = jnp.arange(n, dtype=jnp.float32)
            freqs = t[:, None] * inv_freq[None, :]
            freqs = jnp.concatenate([freqs, freqs], axis=-1)
            base = (half_idx + 0.4 * DIM_HEAD) / (1.4 * DIM_HEAD)
            power = (t - n // 2) / float(WINDOW // 2)
            scale = base[None, :] ** power[:, None]
            scale = jnp.concatenate([scale, scale], axis=-1)
            cos, sin = (jnp.cos(freqs), jnp.sin(freqs))
            q = q * cos * scale + rotate_half(q) * sin * scale
            k = k * cos / scale + rotate_half(k) * sin / scale
            return (q, k)

        def local_attention(q, k, v):
            b, h, n, d = q.shape
            w = n // WINDOW
            bq = q.reshape(b, h, w, WINDOW, d) * QK_SCALE
            bk = k.reshape(b, h, w, WINDOW, d)
            bv = v.reshape(b, h, w, WINDOW, d)

            def look_around(t):
                p = jnp.pad(t, ((0, 0), (0, 0), (1, 0), (0, 0), (0, 0)))
                return jnp.concatenate([p[:, :, :w], p[:, :, 1:]], axis=3)
            bk, bv = (look_around(bk), look_around(bv))
            bt = jnp.arange(n).reshape(w, WINDOW)
            btp = jnp.pad(bt, ((1, 0), (0, 0)), constant_values=-1)
            btk = jnp.concatenate([btp[:w], btp[1:]], axis=1)
            sim = jnp.einsum('bhwid,bhwjd->bhwij', bq, bk)
            i = bt[:, :, None]
            j = btk[:, None, :]
            mask = (i < j) | (i > j + WINDOW) | (j == -1)
            sim = jnp.where(mask, -jnp.finfo(sim.dtype).max, sim)
            attn = jax.nn.softmax(sim, axis=-1)
            out = jnp.einsum('bhwij,bhwjd->bhwid', attn, bv)
            return out.reshape(b, h, n, d)

        def _layer(x, wqkv, qs, ksc, wo, lg, lb, w1, b1, w2, b2):
            b, n, _ = x.shape
            h = shift_token(x)
            qkv = h @ wqkv
            q, k, v = jnp.split(qkv, 3, axis=-1)
            to_heads = lambda t: t.reshape(b, n, HEADS, DIM_HEAD).transpose(0, 2, 1, 3)
            q, k, v = (to_heads(q), to_heads(k), to_heads(v))
            q = l2norm(q) * qs
            k = l2norm(k) * ksc
            q, k = rotary_xpos(q, k)
            o = local_attention(q, k, v)
            o = o.transpose(0, 2, 1, 3).reshape(b, n, INNER)
            x = x + o @ wo
            h = shift_token(x)
            mu = h.mean(-1, keepdims=True)
            var = h.var(-1, keepdims=True)
            h = (h - mu) / jnp.sqrt(var + 1e-05) * lg + lb
            h = h @ w1 + b1
            a, g = jnp.split(h, 2, axis=-1)
            h = a * jax.nn.gelu(g, approximate=False)
            x = x + h @ w2 + b2
            return x
        for l in range(DEPTH):
            x = _layer(x, wqkv[l], q_scale[l], k_scale[l], wo[l], ln_g[l], ln_b[l], w1[l], b1[l], w2[l], b2[l])
        return x
    x = L0_attn_x
    x = x + 0.5 * _L0_ffn_ref(_layernorm(x, axis=-1), L0_ffn_wqkv, L0_ffn_q_scale, L0_ffn_k_scale, L0_ffn_wo, L0_ffn_ln_g, L0_ffn_ln_b, L0_ffn_w1, L0_ffn_b1, L0_ffn_w2, L0_ffn_b2)
    x = x + _L0_attn_ref(_layernorm(x, axis=-1), L0_attn_Wq, L0_attn_bq, L0_attn_Wk, L0_attn_bk, L0_attn_Wv, L0_attn_bv, L0_attn_Wo, L0_attn_bo)
    x = x + 0.5 * _L0_ffn_ref(_layernorm(x, axis=-1), L0_ffn_wqkv, L0_ffn_q_scale, L0_ffn_k_scale, L0_ffn_wo, L0_ffn_ln_g, L0_ffn_ln_b, L0_ffn_w1, L0_ffn_b1, L0_ffn_w2, L0_ffn_b2)
    return x

_drawn_inputs = setup_inputs


def setup_inputs(seed=0):
    import zlib

    import numpy as np

    out = dict(_drawn_inputs(seed))
    spreads = {'L0_ffn_q_scale': (1.0, 0.6),
     'L0_ffn_k_scale': (1.0, 0.6),
     'L0_ffn_ln_g': (1.0, 0.6),
     'L0_ffn_ln_b': (0.0, 0.8),
     'L0_ffn_b1': (0.0, 0.8),
     'L0_ffn_b2': (0.0, 0.1)}
    factors = {'L0_attn_bq': 15.793,
     'L0_attn_bk': 64.0,
     'L0_ffn_wqkv': 2.741,
     'L0_ffn_wo': 2.744,
     'L0_ffn_w1': 5.352,
     'L0_ffn_w2': 5.255}
    for name, (base, spread) in spreads.items():
        noise = np.random.default_rng([zlib.crc32(name.encode()), seed]).standard_normal(out[name].shape)
        drawn = base * np.exp(spread * noise) if base else spread * noise
        out[name] = jnp.asarray(drawn.astype(out[name].dtype))
    for name, factor in factors.items():
        out[name] = (out[name] * factor).astype(out[name].dtype)
    return out
```

```python
from contextlib import ExitStack

import numpy as np

import concourse.bass as bass
from concourse import mybir

F32 = mybir.dt.float32
F32R = mybir.dt.float32r
BF16 = mybir.dt.bfloat16
ALU = mybir.AluOpType
ACT = mybir.ActivationFunctionType
AX = mybir.AxisListType.X

P = 128
SEQS, T, C = 16, 256, 128
TILES = T // P
STREAMS = 4
LAYERS = 2
LOCAL_HEADS, LOCAL_D = 8, 64
WINDOW = 64
INNER = LOCAL_HEADS * LOCAL_D
HID = int(C * 4 * 2 / 3)
FULL_HEADS, FULL_D = 16, 8
PAD_D = 32
CHUNKS = INNER // P
HALF = C // 2
HID_ROWS = [min(P, HID - P * n) for n in range((HID + P - 1) // P)]
HC = len(HID_ROWS)
EPS = 1e-5
NORM_FLOOR = 1e-12
MASKED = -1e30
LOCAL_KEY0 = P - WINDOW
LOCAL_COLS = P + T - LOCAL_KEY0
FULL_COLS = P + T
FULL_SCALE = float(np.float32(1.0) / np.sqrt(np.float32(FULL_D)))
DENSE_BANKS = 3
SCORE_BANKS = 2
PROBS = 4
TURNED = 6
ROPES = 2

PHASES = [("D", "enter"), ("A", 0), ("D", "mid"), ("A", 1), ("D", "to_full"), ("A", "full"),
          ("D", "from_full"), ("A", 0), ("D", "mid"), ("A", 1), ("D", "leave")]
DENSE_LAYER = {"mid": 0, "to_full": 1, "leave": 1}
QKV_LAYER = {"enter": 0, "mid": 1, "from_full": 0}


def heads_of(phase):
    return FULL_HEADS if PHASES[phase][1] == "full" else LOCAL_HEADS


def is_full(phase):
    return PHASES[phase][1] == "full"


DEPTH = 2


def dense_parts(s, ph):
    what = PHASES[ph][1]
    front, back = [], []
    if what == "enter":
        front += [("COPY", s, ph, 0)]
    if what in DENSE_LAYER:
        front += [("WO", s, ph, 0), ("LNH", s, ph, 0), ("NORM", s, ph, 0), ("LNT", s, ph, 0)]
        front += [("W1", s, ph, n) for n in range(HC)] + [("W2", s, ph, 0)]
    if what == "from_full":
        front += [("WOF", s, ph, 0)]
    if what in ("to_full", "from_full", "leave"):
        front += [("XADD", s, ph, 0)]
    if what in ("enter", "to_full", "from_full"):
        front += [("LNX", s, ph, 0), ("NORM", s, ph, 1)]
    if what in ("enter", "from_full"):
        front += [("STATE", s, ph, 0)]
    if what in QKV_LAYER:
        front += [("SPLIT", s, ph, 0)]
        back += [("Q", s, ph, 0), ("Q", s, ph, 1), ("VAL", s, ph, 0), ("Q", s, ph, 2), ("R", s, ph, 0),
                 ("Q", s, ph, 3), ("R", s, ph, 1), ("VAL", s, ph, 1), ("R", s, ph, 2), ("R", s, ph, 3)]
    if what == "to_full":
        front += [("LNT", s, ph, 1)]
        back += [("QF", s, ph, n) for n in range(4)] + [("VALF", s, ph, n) for n in range(TILES)]
    return front, back


SPAN = {"WO": 1.7, "LNH": 1.2, "NORM": 1.6, "LNT": 1.6, "W1": 0.0, "W2": 5.0, "WOF": 1.7, "XADD": 1.5,
        "LNX": 0.5, "STATE": 1.5, "SPLIT": 0.8, "Q": 2.4, "VAL": 0.6, "R": 0.5, "QF": 0.7, "VALF": 0.7, "COPY": 0.5}


def schedule():
    turns = [(s, ph) for ph in range(1, len(PHASES), 2) for s in range(STREAMS)]
    first = [0]
    for _, ph in turns:
        first.append(first[-1] + heads_of(ph))
    first += [first[-1] + LOCAL_HEADS * n for n in (1, 2, 3)]
    placed = []
    for (s, ph), r in zip(turns, first):
        for h in range(heads_of(ph)):
            placed += [(r + h, ("S", s, ph, h)), (r + h + 0.01, ("N", s, ph, h)), (r + h + DEPTH + 0.4, ("T", s, ph, h))]
            if h % 2 == 1:
                placed.append((r + h + DEPTH + 1.7, ("V", s, ph, h // 2)))

    def spread(steps, start, end):
        total = sum(SPAN[x[0]] for x in steps)
        at = 0.0
        for x in steps:
            at += SPAN[x[0]]
            placed.append((start + (end - start) * at / total, x))

    for s in range(STREAMS):
        for ph in range(0, len(PHASES), 2):
            front, back = dense_parts(s, ph)
            if ph == 0:
                end = first[s] - 1
                mid, start = end - LOCAL_HEADS, end - 2 * LOCAL_HEADS
            else:
                start, mid, end = (first[turns.index((s, ph - 1)) + n] + DEPTH + 2 for n in (1, 2, 3))
            spread(front, start, mid - 0.1)
            spread(back, mid, end - 0.1)
    placed.sort(key=lambda x: x[0])
    return [x[1] for x in placed]


DENSE = {"WO", "LNH", "LNT", "W1", "W2", "WOF", "XADD", "STATE", "Q", "VAL", "R", "QF", "VALF"}
ORDER = schedule()
assert len(set(ORDER)) == len(ORDER)

def last_step(kinds, step):
    here = ORDER.index(step)
    for x in reversed(ORDER[:here]):
        if x[0] in kinds and x[1] == step[1]:
            return x
    raise ValueError(step)


def group_done(step):
    return not is_full(step[2]) or step[3] % 2 == 1


def numbered(kinds):
    return {step: n for n, step in enumerate(x for x in ORDER if x[0] in kinds)}


HEAD_NO = numbered({"S"})
DENSE_NO = numbered(DENSE)
ROPE_NO = numbered({"Q"})
HEAD_AT = {n: step for step, n in HEAD_NO.items()}
DENSE_AT = {n: step for step, n in DENSE_NO.items()}
ROPE_AT = {n: step for step, n in ROPE_NO.items()}


LASTS = {"S": 0.75, "T": 0.33, "V": 0.5, "WO": 1.8, "W1": 0.64, "W2": 1.3, "WOF": 1.7, "LNH": 0.2, "LNT": 0.2, "XADD": 0.2,
         "STATE": 0.2, "Q": 0.64, "VAL": 0.64, "VALF": 0.64, "QF": 0.64, "R": 0.43}
AFTER = {"LNH": ({"WO"}, 1.0), "NORM": ({"LNH", "LNX"}, 1.6), "LNT": ({"NORM"}, 1.2), "STATE": ({"NORM"}, 1.2),
         "W1": ({"LNT"}, 1.2), "W2": ({"W1"}, 4.5), "XADD": ({"W2", "WOF"}, 1.1), "LNX": ({"XADD", "COPY"}, 0.6),
         "SPLIT": ({"W2", "STATE"}, 1.2), "Q": ({"SPLIT"}, 0.9), "VAL": ({"SPLIT"}, 0.9), "QF": ({"LNT"}, 1.2),
         "WO": ({"V"}, 0.8), "WOF": ({"V"}, 0.8)}
HOLDS = {"Q": 3.2, "LNH": 4.0, "W1": 5.0}
ACT_LAG = {"S": 1.0, "T": 0.2, "V": 0.2, "STATE": 0.2, "LNT": 0.1, "Q": 0.2, "VAL": 0.3, "VALF": 0.3, "R": 0.2, "QF": 0.2,
           "W1": 0.3}
DVE_LAG = {"S": 0.1, "N": 0.0, "COPY": 0.0, "WO": 0.2, "LNH": 0.2, "LNX": 0.0, "NORM": 0.0, "LNT": 0.6, "W1": 3.0,
           "W2": 0.2, "WOF": 0.2, "XADD": 0.2, "SPLIT": 0.0, "Q": 1.2}
POOL_LAG = {"LNH": 0.0, "LNX": 0.0, "Q": 1.0}


def planned():
    at, now = {}, 0.0
    for step in ORDER:
        kind, s, ph, n = step
        start = now
        if kind in ("N", "T", "R"):
            before, wait = {"N": ("S", 2.2), "T": ("S", 3.2), "R": ("Q", 5.0)}[kind]
            start = max(now, at[(before, s, ph, n)] + wait)
        elif kind == "V":
            start = max(now, at[("T", s, ph, 2 * n + 1)] + 0.7)
        elif kind in AFTER:
            before = last_step(AFTER[kind][0], step)
            start = max(now, at[before] + AFTER[kind][1])
        if kind == "S" and HEAD_NO[step] >= SCORE_BANKS:
            start = max(start, at[HEAD_AT[HEAD_NO[step] - SCORE_BANKS]] + 2.0)
        if kind in DENSE and DENSE_NO[step] >= DENSE_BANKS:
            before = DENSE_AT[DENSE_NO[step] - DENSE_BANKS]
            start = max(start, at[before] + HOLDS.get(before[0], 1.2))
        at[step] = start + LASTS.get(kind, 0.0)
        if kind in LASTS:
            now = at[step]
    for step in ORDER:
        if step[0] == "W1":
            at[step] = at[step[:3] + (HC - 1,)]
    return at


AT = planned()


def in_turn(lag):
    return sorted((x for x in ORDER if x[0] in lag), key=lambda x: AT[x] + lag[x[0]])


def emits(step):
    kind = step[0]
    out = {
        "S": {"scores_ready": 1, "max_ready": 1, "probs_ready": 1},
        "N": {"vector_step": 1, "probs_scaled": 1},
        "T": {"probs_turned": 1, "turned_copied": 1},
        "V": {"heads_summed": 1, "heads_copied": int(kind == "V" and group_done(step))},
        "COPY": {"x_taken": 1},
        "WO": {"state_ready": 1},
        "LNH": {"vector_step": 2, "var_ready": 1, "rstd_ready": 1},
        "LNX": {"vector_step": 2, "var_ready": 1, "rstd_ready": 1},
        "NORM": {"normed": 1},
        "LNT": {"high_ready": 1, "split_ready": 1},
        "W1": {"gelu_ready": 1, "hidden_ready": 1},
        "W2": {"state_ready": 1},
        "WOF": {"state_ready": 1},
        "XADD": {"x_ready": 1},
        "STATE": {"state_set": 1},
        "SPLIT": {"vector_step": 1, "split_ready": 1},
        "Q": {"squares_ready": 1, "squares_summed": 1, "rope_parts": 1, "vector_step": 1, "pool_step": 2, "rope_ready": 1},
        "VAL": {"values_ready": 1},
        "VALF": {"values_ready": 1},
        "R": {"qk_ready": 1},
        "QF": {"qk_ready": 1},
    }[kind].copy()
    if kind in DENSE:
        out["bank_filled"] = 1
    return out


RELEASES = {"WO": "state_ready", "NORM": "normed", "LNT": "split_ready", "W1": "hidden_ready",
            "W2": "state_ready", "WOF": "state_ready", "XADD": "x_ready", "STATE": "state_set",
            "Q": "rope_parts", "VAL": "values_ready", "VALF": "values_ready", "R": "qk_ready",
            "QF": "qk_ready"}


ACT_ORDER = [x for x in in_turn(ACT_LAG) if x[0] != "V" or group_done(x)]
DVE_ORDER = in_turn(DVE_LAG)
POOL_ORDER = in_turn(POOL_LAG)
ORDERS = ((ORDER, ("scores_ready", "probs_turned", "heads_summed", "bank_filled")),
          (ACT_ORDER, ("probs_ready", "turned_copied", "heads_copied", "state_set", "high_ready", "squares_ready",
                       "values_ready", "qk_ready", "gelu_ready")),
          (DVE_ORDER, ("max_ready", "vector_step", "probs_scaled", "x_taken", "state_ready", "var_ready", "normed",
                       "split_ready", "hidden_ready", "x_ready", "squares_summed", "rope_parts")),
          (POOL_ORDER, ("rstd_ready", "pool_step", "rope_ready")))


def tally():
    total, nth = {}, {}
    for order, names in ORDERS:
        for step in order:
            for name, n in emits(step).items():
                if name in names and n:
                    total[name] = total.get(name, 0) + n
                    nth.setdefault(name, {})[step] = total[name]
    return total, nth


TOTAL, NTH = tally()


V_BEFORE = {}
for _step in ORDER:
    if _step[0] == "V":
        V_BEFORE[_step] = next((x for x in reversed(ORDER[:ORDER.index(_step)]) if x[0] == "V" and group_done(x)), None)
LAST = [x for x in DVE_ORDER if x[0] == "XADD"][-1]


def head_no(step):
    return HEAD_NO[("S",) + step[1:]]


def macaron(nc: bass.Bass, a, out):
    with ExitStack() as ctx:
        def sb(name, shape, dt=F32):
            return ctx.enter_context(nc.sbuf_tensor(name, shape, dt))

        def psum(name):
            return ctx.enter_context(nc.psum_tensor(name, [P, 512], F32))

        def sem(name):
            return ctx.enter_context(nc.semaphore(name))

        wqkv_hi = sb("wqkv_hi", [P, LAYERS, 3 * INNER], F32R)
        wqkv_lo = sb("wqkv_lo", [P, LAYERS, 3 * INNER], F32R)
        w1_hi = sb("w1_hi", [P, LAYERS, 2 * HID], F32R)
        w1_lo = sb("w1_lo", [P, LAYERS, 2 * HID], F32R)
        wf_hi = sb("wf_hi", [P, 3, FULL_HEADS * PAD_D], F32R)
        wf_lo = sb("wf_lo", [P, 3, FULL_HEADS * PAD_D], F32R)
        wo = sb("wo", [P, LAYERS, CHUNKS, C])
        w2 = sb("w2", [P, LAYERS, HC, C])
        wof = sb("wof", [P, CHUNKS, C])
        lng = sb("lng", [P, LAYERS])
        lnb = sb("lnb", [P, LAYERS])
        b1 = sb("b1", [P, LAYERS, 2 * HC])
        b1f = sb("b1f", [P, LAYERS, 2 * HC])
        b2 = sb("b2", [P, LAYERS])
        bof = sb("bof", [P, 1])
        biasf = sb("biasf", [P, 3, CHUNKS])
        rope = sb("rope", [P, LAYERS, TILES, 2, 2, LOCAL_D])
        ident = sb("ident", [P, P])
        ident_b = sb("ident_b", [P, P], BF16)
        mask_local = sb("mask_local", [P, LOCAL_COLS], BF16)
        mask_full = sb("mask_full", [P, FULL_COLS], BF16)
        neg_half = sb("neg_half", [P, LOCAL_HEADS])
        neg_max = sb("neg_max", [P, PROBS, TILES])
        prob_sum = sb("prob_sum", [P, PROBS, TILES])
        prob_inv = sb("prob_inv", [P, PROBS, TILES])
        probs_local = sb("probs_local", [P, PROBS, P + T])

        def per_stream(name, shape, dt=F32):
            return [sb(f"{name}{s}", shape, dt) for s in range(STREAMS)]

        x_in = per_stream("x_in", [P, TILES, C])
        x_sb = per_stream("x_sb", [P, TILES, C])
        state = per_stream("state", [P, T + 1])
        y_t = per_stream("y_t", [P, T])

        with ExitStack() as setup:
            def staged(name, shape):
                return setup.enter_context(nc.sbuf_tensor(name, shape, F32))

            stage = staged("stage", [P, LAYERS, 3 * INNER])
            stage1 = staged("stage1", [P, LAYERS, 2 * HID])
            scaled1 = staged("scaled1", [P, LAYERS, 2 * HID])
            stagef = staged("stagef", [P, 3, C])
            padded = staged("padded", [P, 3, FULL_HEADS, PAD_D])
            rope_in = staged("rope_in", [P, TILES, 2, 2, LOCAL_D])
            qk_scale = staged("qk_scale", [P, 2, LAYERS, LOCAL_D])

        normal = per_stream("normal", [P, TILES, C])
        bn = per_stream("bn", [P, TILES, 6])
        mean_var = per_stream("mean_var", [P, TILES, 2])
        var_eps = per_stream("var_eps", [P, TILES])
        rstd = per_stream("rstd", [P, TILES])
        q_t = per_stream("q_t", [P, CHUNKS, T])
        o_t = q_t
        k_t = per_stream("k_t", [P, CHUNKS, T])
        val = per_stream("val", [P, TILES, INNER])

        h_hi = [sb(f"h_hi{n}", [P, T], F32R) for n in range(2)] * (STREAMS // 2)
        h_lo = [sb(f"h_lo{n}", [P, T], F32R) for n in range(2)] * (STREAMS // 2)
        gelu = sb("gelu", [P, HC, T])
        hidden = sb("hidden", [P, HC, T])
        squares = sb("squares", [P, ROPES, INNER])
        sums = sb("sums", [P, ROPES, LOCAL_HEADS])
        sums_floor = sb("sums_floor", [P, ROPES, LOCAL_HEADS])
        rnorm = sb("rnorm", [P, ROPES, LOCAL_HEADS])
        part_cos = sb("part_cos", [P, ROPES, INNER])
        part_sin = sb("part_sin", [P, ROPES, INNER])
        roped_raw = part_cos
        roped = sb("roped", [P, ROPES, INNER])
        probs_full = sb("probs_full", [P, PROBS, P + T])
        turned = sb("turned", [P, TURNED, P + T])

        ps_scores = [psum(f"ps_scores{n}") for n in range(SCORE_BANKS)]
        ps_turned = [psum(f"ps_turned{n}") for n in range(2)]
        ps_heads = psum("ps_heads")
        ps_dense = [psum(f"ps_dense{n}") for n in range(DENSE_BANKS)]

        w_loaded = sem("w_loaded")
        f_loaded = sem("f_loaded")
        x_loaded = [sem(f"x_loaded{s}") for s in range(STREAMS)]
        stored = [sem(f"stored{s}") for s in range(STREAMS)]
        cleared = sem("cleared")
        pads_cleared = sem("pads_cleared")
        fold_summed = sem("fold_summed")
        setup_step = sem("setup_step")
        weights_ready = sem("weights_ready")
        sems = {name: sem(name) for name in TOTAL}

        def count(i, name, step, back=0):
            return i * TOTAL[name] + (NTH[name][step] - back)

        block = ctx.enter_context(nc.Block())

        x_dram = a["L0_attn_x"].rearrange("(n s) (t p) c -> n s p t c", s=STREAMS, p=P)
        out_dram = out.rearrange("(n s) (t p) c -> n s p t c", s=STREAMS, p=P)
        ITERS = SEQS // STREAMS
        N_WLOADS = 1 + 2 * LAYERS + 3 + LAYERS * (3 + 2 * HC) + 4
        N_FLOADS = 4 * P // PAD_D
        N_SELECTS = 8

        def w1_cols(n):
            at = P * (n % HC) + (HID if n >= HC else 0)
            return at, HID_ROWS[n % HC]

        @block.sync
        def _(sp):
            def load_x(n, s):
                sp.dma_start(x_in[s][:], x_dram[n, s]).then_inc(x_loaded[s], 16)

            for s in range(STREAMS):
                load_x(0, s)
            n = 0

            def load(dst, src):
                sp.dma_start(dst, src).then_inc(w_loaded, 16)
                return 1

            with nc.allow_non_contiguous_dma(reason="bias columns, once"):
                n += load(rope_in[:], a["rope"].rearrange("(t p) a b d -> p t a b d", p=P))
                for m, name in enumerate(("L0_ffn_q_scale", "L0_ffn_k_scale")):
                    for l in range(LAYERS):
                        src = a[name][l:l + 1].to_broadcast([P, LOCAL_D])
                        sp.dma_start(qk_scale[:, m, l], src).then_inc(stored[2 * m + l], 16)
                for l in range(LAYERS):
                    n += load(stage[:, l], a["L0_ffn_wqkv"][l])
                    n += load(stage1[:, l], a["L0_ffn_w1"][l])
                for m, w in enumerate(("L0_attn_Wq", "L0_attn_Wk", "L0_attn_Wv")):
                    n += load(stagef[:, m], a[w])
                for l in range(LAYERS):
                    n += load(wo[:, l], a["L0_ffn_wo"][l].rearrange("(c p) n -> p c n", p=P))
                    full = HID // P
                    n += load(w2[:, l, 0:full], a["L0_ffn_w2"][l, 0:full * P].rearrange("(c p) n -> p c n", p=P))
                    n += load(w2[0:HID_ROWS[-1], l, full], a["L0_ffn_w2"][l, full * P:HID])
                    for m in range(2 * HC):
                        at, rows = w1_cols(m)
                        n += load(b1[0:rows, l, m:m + 1], a["L0_ffn_b1"][l, at:at + rows].rearrange("(p o) -> p o", o=1))
                for dst, src in ((lng, "L0_ffn_ln_g"), (lnb, "L0_ffn_ln_b"), (b2, "L0_ffn_b2")):
                    n += load(dst[:], a[src].rearrange("l p -> p l"))
                n += load(bof[:], a["L0_attn_bo"].rearrange("(p o) -> p o", o=1))
                assert n == N_WLOADS, n
                sp.wait_ge(pads_cleared, 1)
                m = 0
                for j in range(P // PAD_D):
                    rows = slice(PAD_D * j, PAD_D * j + FULL_D)
                    for b, name in enumerate(("L0_attn_bq", "L0_attn_bk", "L0_attn_bv")):
                        sp.dma_start(biasf[rows, b, :], a[name].rearrange("(c j d) -> j d c", j=4, d=FULL_D)[j]).then_inc(f_loaded, 16)
                        m += 1
                    sp.dma_start(wof[rows], a["L0_attn_Wo"].rearrange("(c j d) n -> j d c n", j=4, d=FULL_D)[j]).then_inc(f_loaded, 16)
                    m += 1
                assert m == N_FLOADS

            def store(i, s):
                sp.wait_ge(sems["x_ready"], count(i, "x_ready", ("XADD", s, len(PHASES) - 1, 0)))
                sp.dma_start(out_dram[i, s], x_sb[s][:]).then_inc(stored[s], 16)

            with sp.Fori(0, ITERS - 1) as i:
                for s in range(STREAMS):
                    sp.wait_ge(sems["x_taken"], count(i, "x_taken", ("COPY", s, 0, 0)))
                    load_x(i + 1, s)
                for s in range(STREAMS):
                    store(i, s)
            for s in range(STREAMS):
                store(ITERS - 1, s)
            for s in range(STREAMS):
                sp.wait_ge(stored[s], 16 * (ITERS + 1))

        @block.gpsimd
        def _(pool):
            nc.gpsimd.memset(padded[:], 0.0)
            nc.gpsimd.memset(biasf[:], 0.0)
            nc.gpsimd.memset(wof[:], 0.0).then_inc(pads_cleared, 1)
            nc.gpsimd.memset(ident[:], 0.0)
            nc.gpsimd.memset(ident_b[:], 0.0)
            nc.gpsimd.memset(mask_local[:], 0.0)
            nc.gpsimd.memset(mask_full[:], 0.0)
            nc.gpsimd.memset(neg_half[:], -0.5)
            nc.gpsimd.memset(probs_local[:], 0.0).then_inc(cleared, 1)
            pool.wait_ge(cleared, 1)
            n = 1

            def select(t, base, step, chan, op, fill):
                nonlocal n
                nc.gpsimd.affine_select(out=t, in_=t, compare_op=op, fill=fill, base=base,
                                        pattern=[[step, t.shape[1]]], channel_multiplier=chan).then_inc(cleared, 1)
                n += 1
                pool.wait_ge(cleared, n)

            select(ident[:], 0, -1, 1, ALU.not_equal, 1.0)
            select(ident_b[:], 0, -1, 1, ALU.not_equal, 1.0)
            select(mask_local[:, 0:P], 0, -1, 1, ALU.is_ge, MASKED)
            select(mask_local[:, 0:P], WINDOW, 1, -1, ALU.is_ge, MASKED)
            select(mask_local[:, P:], 0, 1, -1, ALU.is_ge, MASKED)
            select(mask_local[:, P:], WINDOW, -1, 1, ALU.is_ge, MASKED)
            select(mask_full[:, 0:P], 0, -1, 1, ALU.is_ge, MASKED)
            select(mask_full[:, P:], P, -1, 1, ALU.is_ge, MASKED)
            assert n == 1 + N_SELECTS

            def norm_scale(i, step):
                s = step[1]
                pool.wait_ge(sems["var_ready"], count(i, "var_ready", step))
                nc.gpsimd.tensor_tensor(rstd[s][:], var_eps[s][:], neg_half[:, 0:TILES], ALU.pow).then_inc(sems["rstd_ready"], 1)

            def rope_join(i, step):
                u = ROPE_NO[step] % ROPES
                pool.wait_ge(sems["squares_summed"], count(i, "squares_summed", step))
                nc.gpsimd.tensor_tensor(rnorm[:, u], sums_floor[:, u], neg_half[:], ALU.pow).then_inc(sems["pool_step"], 1)
                pool.wait_ge(sems["rope_parts"], count(i, "rope_parts", step))
                nc.gpsimd.tensor_tensor(roped_raw[:, u], part_cos[:, u], part_sin[:, u], ALU.add).then_inc(sems["pool_step"], 1)
                if ROPE_NO[step] >= ROPES:
                    before = ROPE_AT[ROPE_NO[step] - ROPES]
                    pool.wait_ge(sems["bank_filled"], count(i, "bank_filled", ("R",) + before[1:]))
                pool.wait_ge(sems["pool_step"], count(i, "pool_step", step))
                nc.gpsimd.tensor_tensor(roped[:, u].rearrange("p (h d) -> p h d", d=LOCAL_D),
                                        roped_raw[:, u].rearrange("p (h d) -> p h d", d=LOCAL_D),
                                        rnorm[:, u].rearrange("p (h o) -> p h o", o=1).to_broadcast([P, LOCAL_HEADS, LOCAL_D]),
                                        ALU.mult).then_inc(sems["rope_ready"], 1)

            with pool.Fori(0, ITERS) as i:
                for step in POOL_ORDER:
                    if step[0] == "Q":
                        rope_join(i, step)
                    else:
                        norm_scale(i, step)
                pool.wait_ge(sems["x_ready"], count(i, "x_ready", LAST))

        @block.scalar
        def _(act):
            def exp_scores(i, step):
                s, ph = step[1:3]
                g = HEAD_NO[step]
                u, bank = g % PROBS, ps_scores[g % SCORE_BANKS]
                act.wait_ge(sems["max_ready"], count(i, "max_ready", step))
                if g >= PROBS:
                    act.wait_ge(sems["probs_turned"], count(i, "probs_turned", ("T",) + HEAD_AT[g - PROBS][1:]))
                probs, at = (probs_full, P) if is_full(ph) else (probs_local, P + LOCAL_KEY0)
                cols = FULL_COLS if is_full(ph) else LOCAL_COLS
                for t, (dst, src) in enumerate(((probs[:, u, 0:P], bank[:, 0:P]),
                                                (probs[:, u, at:P + T], bank[:, P:cols]))):
                    last = nc.scalar.activation(dst, src, ACT.Exp, bias=neg_max[:, u, t:t + 1],
                                                accum_out=prob_sum[:, u, t:t + 1])
                last.then_inc(sems["probs_ready"], 1)

            def copy_turned(i, step):
                g = head_no(step)
                act.wait_ge(sems["probs_turned"], count(i, "probs_turned", step))
                if g >= TURNED:
                    h = HEAD_AT[g - TURNED]
                    act.wait_ge(sems["heads_summed"], count(i, "heads_summed", ("V", h[1], h[2], h[3] // 2)))
                cols = FULL_COLS if is_full(step[2]) else LOCAL_COLS
                nc.scalar.activation(turned[:, g % TURNED, 0:cols], ps_turned[g % 2][:, 0:cols],
                                     ACT.Copy).then_inc(sems["turned_copied"], 1)

            def copy_heads(i, step):
                s, ph, n = step[1:]
                act.wait_ge(sems["heads_summed"], count(i, "heads_summed", step))
                if is_full(ph):
                    c = n // 2
                    nc.scalar.activation(o_t[s][:, c], ps_heads[:, 0:T], ACT.Identity,
                                         bias=biasf[:, 2, c:c + 1]).then_inc(sems["heads_copied"], 1)
                else:
                    nc.scalar.activation(o_t[s][:, n], ps_heads[:, 0:T], ACT.Copy).then_inc(sems["heads_copied"], 1)

            def dense(i, step):
                kind, s, ph, n = step
                bank = ps_dense[DENSE_NO[step] % DENSE_BANKS]
                act.wait_ge(sems["bank_filled"], count(i, "bank_filled", step))
                if kind == "STATE":
                    nc.scalar.activation(state[s][0:HALF, 0:T], bank[0:HALF, 0:T], ACT.Copy)
                    nc.scalar.activation(state[s][HALF:C, 1:T + 1], bank[HALF:C, 0:T], ACT.Copy).then_inc(sems["state_set"], 1)
                if kind == "LNT":
                    nc.scalar.activation(h_hi[s][:], bank[:, 0:T], ACT.Copy).then_inc(sems["high_ready"], 1)
                if kind == "Q":
                    u = ROPE_NO[step]
                    if u >= ROPES:
                        act.wait_ge(sems["squares_summed"], count(i, "squares_summed", ROPE_AT[u - ROPES]))
                    nc.scalar.activation(squares[:, u % ROPES], bank[:], ACT.Square).then_inc(sems["squares_ready"], 1)
                if kind in ("VAL", "VALF"):
                    nc.scalar.activation(val[s][:, n], bank[:], ACT.Copy).then_inc(sems["values_ready"], 1)
                if kind == "R":
                    dst = (q_t if n % 2 == 0 else k_t)[s]
                    nc.scalar.activation(dst[:, :, P * (n // 2):P * (n // 2 + 1)],
                                         bank[:].rearrange("p (c q) -> p c q", c=CHUNKS), ACT.Copy).then_inc(sems["qk_ready"], 1)
                if kind == "QF":
                    dst, scale = ((q_t, FULL_SCALE), (k_t, 1.0))[n // 2]
                    for m in range(2):
                        c = 2 * (n % 2) + m
                        last = nc.scalar.activation(dst[s][:, c], bank[:, T * m:T * (m + 1)], ACT.Identity,
                                                    bias=biasf[:, n // 2, c:c + 1], scale=scale)
                    last.then_inc(sems["qk_ready"], 1)
                if kind == "W1":
                    l, rows = DENSE_LAYER[PHASES[ph][1]], HID_ROWS[n]
                    nc.scalar.activation(gelu[0:rows, n], bank[0:rows, 0:T], ACT.Gelu,
                                         bias=b1f[0:rows, l, HC + n:HC + n + 1]).then_inc(sems["gelu_ready"], 1)

            act.wait_ge(weights_ready, 1)
            with act.Fori(0, ITERS) as i:
                for step in ACT_ORDER:
                    if step[0] == "S":
                        exp_scores(i, step)
                    elif step[0] == "T":
                        copy_turned(i, step)
                    elif step[0] == "V":
                        copy_heads(i, step)
                    else:
                        dense(i, step)
                act.wait_ge(sems["x_ready"], count(i, "x_ready", LAST))

        @block.vector
        def _(dve):
            links = [0]

            def link(ins):
                links[0] += 1
                ins.then_inc(setup_step, 1)
                dve.wait_ge(setup_step, links[0])

            dve.wait_ge(w_loaded, 16 * N_WLOADS)
            for s in range(STREAMS):
                dve.wait_ge(stored[s], 16)
            dve.wait_ge(pads_cleared, 1)
            for s in range(STREAMS):
                nc.vector.memset(state[s][HALF:C, 0:1], 0.0)
            for l in range(LAYERS):
                nc.vector.tensor_copy(wqkv_hi[:, l], stage[:, l])
                nc.vector.tensor_scalar(scaled1[:, l], stage1[:, l], lng[:, l:l + 1], None, ALU.mult)
                for t in range(TILES):
                    sc = qk_scale[:, :, l]
                    nc.vector.tensor_tensor(rope[:, l, t, 0], rope_in[:, t, 0], sc, ALU.mult)
                    hd = LOCAL_D // 2
                    nc.vector.tensor_tensor(rope[:, l, t, 1, :, 0:hd], rope_in[:, t, 1, :, 0:hd], sc[:, :, hd:], ALU.mult)
                    last = nc.vector.tensor_tensor(rope[:, l, t, 1, :, hd:], rope_in[:, t, 1, :, hd:], sc[:, :, 0:hd], ALU.mult)
            for m in range(3):
                last = nc.vector.tensor_copy(padded[:, m, :, 0:FULL_D], stagef[:, m].rearrange("p (h d) -> p h d", d=FULL_D))
            link(last)
            nc.vector.tensor_copy(wf_hi[:], padded[:].rearrange("p m h d -> p m (h d)"))
            link(nc.vector.tensor_copy(w1_hi[:], scaled1[:]))
            for l in range(LAYERS):
                nc.vector.tensor_tensor(wqkv_lo[:, l], stage[:, l], wqkv_hi[:, l].bitcast(F32), ALU.subtract)
            nc.vector.tensor_tensor(w1_lo[:], scaled1[:], w1_hi[:].bitcast(F32), ALU.subtract)
            nc.vector.tensor_tensor(wf_lo[:], padded[:].rearrange("p m h d -> p m (h d)"), wf_hi[:].bitcast(F32), ALU.subtract)
            dve.wait_ge(fold_summed, 1)
            for l in range(LAYERS):
                for m in range(2 * HC):
                    rows = w1_cols(m)[1]
                    nc.vector.tensor_tensor(b1f[0:rows, l, m:m + 1], b1[0:rows, l, m:m + 1],
                                            ps_heads[0:rows, 2 * HC * l + m:2 * HC * l + m + 1], ALU.add)
            dve.wait_ge(f_loaded, 16 * N_FLOADS)
            nc.vector.tensor_scalar(biasf[:, 0], biasf[:, 0], FULL_SCALE, None, ALU.mult).then_inc(weights_ready, 1)
            dve.wait_ge(weights_ready, 1)
            dve.wait_ge(cleared, 1 + N_SELECTS)

            def row_max(i, step):
                g = HEAD_NO[step]
                u, bank = g % PROBS, ps_scores[g % SCORE_BANKS]
                cols = FULL_COLS if is_full(step[2]) else LOCAL_COLS
                dve.wait_ge(sems["scores_ready"], count(i, "scores_ready", step))
                nc.vector.tensor_reduce(neg_max[:, u, 0:1], bank[:, 0:P], AX, ALU.max, negate=True)
                nc.vector.tensor_reduce(neg_max[:, u, 1:2], bank[:, P:cols], AX, ALU.max,
                                        negate=True).then_inc(sems["max_ready"], 1)

            def scale_probs(i, step):
                u = head_no(step) % PROBS
                probs, at = (probs_full, P) if is_full(step[2]) else (probs_local, P + LOCAL_KEY0)
                dve.wait_ge(sems["probs_ready"], count(i, "probs_ready", ("S",) + step[1:]))
                nc.vector.reciprocal(prob_inv[:, u], prob_sum[:, u]).then_inc(sems["vector_step"], 1)
                dve.wait_ge(sems["vector_step"], count(i, "vector_step", step))
                nc.vector.tensor_scalar(probs[:, u, 0:P], probs[:, u, 0:P], prob_inv[:, u, 0:1], None, ALU.mult)
                nc.vector.tensor_scalar(probs[:, u, at:P + T], probs[:, u, at:P + T], prob_inv[:, u, 1:2], None,
                                        ALU.mult).then_inc(sems["probs_scaled"], 1)

            def layer_norm(i, step, source):
                s = step[1]
                for t in range(TILES):
                    last = nc.vector.bn_stats(bn[s][:, t], source[t])
                last.then_inc(sems["vector_step"], 1)
                dve.wait_ge(sems["vector_step"], count(i, "vector_step", step, 1))
                nc.vector.memset(var_eps[s][:], 0.0)
                for t in range(TILES):
                    last = nc.vector.bn_aggr(mean_var[s][:, t], bn[s][:, t])
                last.then_inc(sems["vector_step"], 1)
                dve.wait_ge(sems["vector_step"], count(i, "vector_step", step))
                nc.vector.tensor_scalar(var_eps[s][:], mean_var[s][:, :, 1], EPS, None, ALU.add).then_inc(sems["var_ready"], 1)

            def normalise(i, step, source):
                s = step[1]
                dve.wait_ge(sems["rstd_ready"], count(i, "rstd_ready", last_step({"LNH", "LNX"}, step)))
                for t in range(TILES):
                    last = nc.vector.tensor_scalar(normal[s][:, t], source[t], mean_var[s][:, t, 0:1], rstd[s][:, t:t + 1],
                                                   ALU.subtract, ALU.mult)
                last.then_inc(sems["normed"], 1)

            def add_to_state(s, bank, dst, bias):
                for rows, at in ((slice(0, HALF), 0), (slice(HALF, C), 1)):
                    old = state[s][rows, at:at + T]
                    new = dst[rows, :] if dst is not None else old
                    if bias is None:
                        last = nc.vector.tensor_tensor(new, bank[rows, 0:T], old, ALU.add)
                    else:
                        last = nc.vector.scalar_tensor_tensor(out=new, in0=bank[rows, 0:T], scalar=bias[rows], in1=old,
                                                              op0=ALU.add, op1=ALU.add)
                last.then_inc(sems["state_ready"], 1)

            def dense(i, step):
                kind, s, ph, n = step
                bank = ps_dense[DENSE_NO[step] % DENSE_BANKS] if kind in DENSE else None
                what = PHASES[ph][1]
                if kind == "COPY":
                    dve.wait_ge(x_loaded[s], i * 16 + 16)
                    dve.wait_ge(stored[s], i * 16 + 16)
                    nc.vector.tensor_copy(x_sb[s][:], x_in[s][:]).then_inc(sems["x_taken"], 1)
                elif kind == "LNX":
                    before = last_step({"XADD", "COPY"}, step)
                    name = "x_taken" if before[0] == "COPY" else "x_ready"
                    dve.wait_ge(sems[name], count(i, name, before))
                    layer_norm(i, step, [x_sb[s][:, t] for t in range(TILES)])
                elif kind == "NORM":
                    before = last_step({"LNH", "LNX"}, step)
                    if before[0] == "LNH":
                        bank = ps_dense[DENSE_NO[before] % DENSE_BANKS]
                        normalise(i, step, [bank[:, P * t:P * (t + 1)] for t in range(TILES)])
                    else:
                        normalise(i, step, [x_sb[s][:, t] for t in range(TILES)])
                elif kind == "SPLIT":
                    if last_step({"STATE", "W2"}, step)[0] == "STATE":
                        dve.wait_ge(sems["state_set"], count(i, "state_set", last_step({"STATE"}, step)))
                    else:
                        dve.wait_ge(sems["state_ready"], count(i, "state_ready", last_step({"W2"}, step)))
                    nc.vector.tensor_copy(h_hi[s][:], state[s][:, 0:T]).then_inc(sems["vector_step"], 1)
                    dve.wait_ge(sems["vector_step"], count(i, "vector_step", step))
                    nc.vector.tensor_tensor(h_lo[s][:], state[s][:, 0:T], h_hi[s][:].bitcast(F32),
                                            ALU.subtract).then_inc(sems["split_ready"], 1)
                elif kind == "LNT":
                    dve.wait_ge(sems["high_ready"], count(i, "high_ready", step))
                    nc.vector.tensor_tensor(h_lo[s][:], bank[:, 0:T], h_hi[s][:].bitcast(F32),
                                            ALU.subtract).then_inc(sems["split_ready"], 1)
                elif kind == "Q":
                    u, t, m = ROPE_NO[step], n // 2, n % 2
                    table = rope[:, QKV_LAYER[what], t]
                    dve.wait_ge(sems["squares_ready"], count(i, "squares_ready", step))
                    if u >= ROPES:
                        dve.wait_ge(sems["rope_ready"], count(i, "rope_ready", ROPE_AT[u - ROPES]))
                    u %= ROPES
                    nc.vector.tensor_reduce(sums[:, u], squares[:, u].rearrange("p (h d) -> p h d", d=LOCAL_D), AX,
                                            ALU.add).then_inc(sems["vector_step"], 1)
                    nc.vector.tensor_tensor(part_cos[:, u].rearrange("p (h d) -> p h d", d=LOCAL_D),
                                            bank[:].rearrange("p (h d) -> p h d", d=LOCAL_D),
                                            table[:, 0, m:m + 1].to_broadcast([P, LOCAL_HEADS, LOCAL_D]), ALU.mult)
                    dve.wait_ge(sems["vector_step"], count(i, "vector_step", step))
                    nc.vector.tensor_scalar(sums_floor[:, u], sums[:, u], NORM_FLOOR * NORM_FLOOR, None,
                                            ALU.max).then_inc(sems["squares_summed"], 1)
                    hd = LOCAL_D // 2
                    for half in range(2):
                        dst, src = hd * half, hd * (1 - half)
                        last = nc.vector.tensor_tensor(
                            part_sin[:, u].rearrange("p (h d) -> p h d", d=LOCAL_D)[:, :, dst:dst + hd],
                            bank[:].rearrange("p (h d) -> p h d", d=LOCAL_D)[:, :, src:src + hd],
                            table[:, 1, m:m + 1, dst:dst + hd].to_broadcast([P, LOCAL_HEADS, hd]), ALU.mult)
                    last.then_inc(sems["rope_parts"], 1)
                elif kind == "W1":
                    l, rows = DENSE_LAYER[what], HID_ROWS[n]
                    dve.wait_ge(sems["gelu_ready"], count(i, "gelu_ready", step))
                    nc.vector.scalar_tensor_tensor(out=hidden[0:rows, n], in0=bank[0:rows, T:2 * T],
                                                   scalar=b1f[0:rows, l, n:n + 1], in1=gelu[0:rows, n],
                                                   op0=ALU.add, op1=ALU.mult).then_inc(sems["hidden_ready"], 1)
                else:
                    dve.wait_ge(sems["bank_filled"], count(i, "bank_filled", step))
                    if kind == "WO":
                        add_to_state(s, bank, None, None)
                    if kind == "LNH":
                        layer_norm(i, step, [bank[:, P * t:P * (t + 1)] for t in range(TILES)])
                    if kind == "W2":
                        l = DENSE_LAYER[what]
                        add_to_state(s, bank, y_t[s] if l == LAYERS - 1 else None, b2[:, l:l + 1])
                    if kind == "WOF":
                        nc.vector.tensor_scalar(y_t[s][:], bank[:, 0:T], bof[:, 0:1], None, ALU.add).then_inc(sems["state_ready"], 1)
                    if kind == "XADD":
                        nc.vector.scalar_tensor_tensor(out=x_sb[s][:].rearrange("p t c -> p (t c)"), in0=bank[:, 0:T],
                                                       scalar=1.0 if what == "from_full" else 0.5,
                                                       in1=x_sb[s][:].rearrange("p t c -> p (t c)"),
                                                       op0=ALU.mult, op1=ALU.add).then_inc(sems["x_ready"], 1)

            with dve.Fori(0, ITERS) as i:
                for step in DVE_ORDER:
                    if step[0] == "S":
                        row_max(i, step)
                    elif step[0] == "N":
                        scale_probs(i, step)
                    else:
                        dense(i, step)

        @block.tensor
        def _(pe):
            pe.wait_ge(w_loaded, 16 * N_WLOADS)
            for l in range(LAYERS):
                for m in range(2 * HC):
                    at, rows = w1_cols(m)
                    last = nc.tensor.matmul(ps_heads[0:rows, 2 * HC * l + m:2 * HC * l + m + 1], stage1[:, l, at:at + rows],
                                            lnb[:, l:l + 1], start=True, stop=True)
            last.then_inc(fold_summed, 1)
            pe.wait_ge(weights_ready, 1)
            pe.wait_ge(cleared, 1 + N_SELECTS)

            def split_matmul(dst, hi, lo, w_hi, w_lo, moving_weights):
                for n, (h, w) in enumerate(((hi, w_hi), (lo, w_hi), (hi, w_lo))):
                    lhs, rhs = (h, w) if moving_weights else (w, h)
                    last = nc.tensor.matmul(dst, lhs, rhs, start=(n == 0), stop=(n == 2))
                return last

            def scores(i, step):
                _, s, ph, h = step
                g = HEAD_NO[step]
                bank = ps_scores[g % SCORE_BANKS]
                if h == 0:
                    pe.wait_ge(sems["qk_ready"], count(i, "qk_ready", last_step({"R", "QF"}, step)))
                if g >= SCORE_BANKS:
                    pe.wait_ge(sems["probs_ready"], count(i, "probs_ready", HEAD_AT[g - SCORE_BANKS]))
                if is_full(ph):
                    cols, mask, per, rows, key0 = FULL_COLS, mask_full, P // PAD_D, FULL_D, 0
                    at = PAD_D * (h % per)
                else:
                    cols, mask, per, rows, key0 = LOCAL_COLS, mask_local, 2, LOCAL_D, LOCAL_KEY0
                    at = LOCAL_D * (h % per)
                q, k = q_t[s][at:at + rows, h // per], k_t[s][at:at + rows, h // per]
                for part, tok, keys in ((slice(0, P), slice(0, P), slice(0, P)), (slice(P, cols), slice(P, T), slice(key0, T))):
                    nc.tensor.matmul(bank[:, part], ident_b[:], mask[:, part], start=True, stop=False)
                    last = nc.tensor.matmul(bank[:, part], q[:, tok], k[:, keys], start=False, stop=True)
                last.then_inc(sems["scores_ready"], 1)

            def turn(i, step):
                g = head_no(step)
                bank, u = ps_turned[g % 2], g % PROBS
                if g >= 2:
                    pe.wait_ge(sems["turned_copied"], count(i, "turned_copied", ("T",) + HEAD_AT[g - 2][1:]))
                pe.wait_ge(sems["probs_scaled"], count(i, "probs_scaled", ("N",) + step[1:]))
                if is_full(step[2]):
                    for n in range(3):
                        last = nc.tensor.transpose(bank[:, P * n:P * (n + 1)], probs_full[:, u, P * n:P * (n + 1)], ident[:])
                else:
                    nc.tensor.transpose(bank[:, 0:P], probs_local[:, u, 0:P], ident[:])
                    nc.tensor.transpose(bank[:, P:P + WINDOW], probs_local[0:WINDOW, u, P:2 * P], ident[0:WINDOW, 0:WINDOW])
                    last = nc.tensor.transpose(bank[:, P + WINDOW:LOCAL_COLS], probs_local[:, u, 2 * P:3 * P], ident[:])
                last.then_inc(sems["probs_turned"], 1)

            def values(i, step):
                _, s, ph, n = step
                full = is_full(ph)
                pe.wait_ge(sems["turned_copied"], count(i, "turned_copied", ("T", s, ph, 2 * n + 1)))
                if n == 0:
                    pe.wait_ge(sems["values_ready"], count(i, "values_ready", last_step({"VAL", "VALF"}, step)))
                first = not full or n % 2 == 0
                if first and V_BEFORE[step] is not None:
                    pe.wait_ge(sems["heads_copied"], count(i, "heads_copied", V_BEFORE[step]))
                d = PAD_D if full else LOCAL_D
                k0 = T if full else P + WINDOW
                for t in range(TILES):
                    for h in (2 * n, 2 * n + 1):
                        at = d * (h % (P // d))
                        g = HEAD_NO[("S", s, ph, h)] % TURNED
                        cols, q0 = ((0, k0), 0) if t == 0 else ((k0, k0 + P), P)
                        last = nc.tensor.matmul(ps_heads[at:at + d, q0:q0 + cols[1] - cols[0]],
                                                val[s][:, t, d * h:d * (h + 1)], turned[:, g, cols[0]:cols[1]],
                                                start=(t == 0), stop=(t == TILES - 1), skip_group_check=True)
                last.then_inc(sems["heads_summed"], 1)

            def dense(i, step):
                kind, s, ph, n = step
                what = PHASES[ph][1]
                no = DENSE_NO[step]
                bank = ps_dense[no % DENSE_BANKS]
                if no >= DENSE_BANKS:
                    before = DENSE_AT[no - DENSE_BANKS]
                    if before[0] == "LNH":
                        before = ("NORM",) + before[1:]
                    pe.wait_ge(sems[RELEASES[before[0]]], count(i, RELEASES[before[0]], before))
                if kind in ("WO", "WOF"):
                    pe.wait_ge(sems["heads_copied"], count(i, "heads_copied", last_step({"V"}, step)))
                    w = wof if kind == "WOF" else wo[:, DENSE_LAYER[what]]
                    for c in range(CHUNKS):
                        last = nc.tensor.matmul(bank[:, 0:T], w[:, c], o_t[s][:, c], start=(c == 0), stop=(c == CHUNKS - 1))
                if kind == "LNH":
                    pe.wait_ge(sems["state_ready"], count(i, "state_ready", last_step({"WO"}, step)))
                    for t in range(TILES):
                        last = nc.tensor.transpose(bank[:, P * t:P * (t + 1)], state[s][:, P * t:P * (t + 1)], ident[:])
                if kind in ("LNT", "STATE"):
                    pe.wait_ge(sems["normed"], count(i, "normed", last_step({"NORM"}, step)))
                    for t in range(TILES):
                        last = nc.tensor.transpose(bank[:, P * t:P * (t + 1)], normal[s][:, t], ident[:])
                if kind == "XADD":
                    pe.wait_ge(sems["state_ready"], count(i, "state_ready", last_step({"W2", "WOF"}, step)))
                    for t in range(TILES):
                        last = nc.tensor.transpose(bank[:, P * t:P * (t + 1)], y_t[s][:, P * t:P * (t + 1)], ident[:])
                if kind in ("W1", "Q", "VAL", "QF", "VALF"):
                    pe.wait_ge(sems["split_ready"], count(i, "split_ready", last_step({"SPLIT", "LNT"}, step)))
                hi, lo = h_hi[s], h_lo[s]
                if kind == "W1":
                    l = DENSE_LAYER[what]
                    for m, at0 in ((HC + n, 0), (n, T)):
                        at, rows = w1_cols(m)
                        last = split_matmul(bank[0:rows, at0:at0 + T], hi[:], lo[:], w1_hi[:, l, at:at + rows],
                                            w1_lo[:, l, at:at + rows], False)
                if kind == "W2":
                    pe.wait_ge(sems["hidden_ready"], count(i, "hidden_ready", last_step({"W1"}, step)))
                    l = DENSE_LAYER[what]
                    for c, rows in enumerate(HID_ROWS):
                        last = nc.tensor.matmul(bank[:, 0:T], w2[0:rows, l, c], hidden[0:rows, c], start=(c == 0), stop=(c == HC - 1))
                if kind in ("Q", "VAL"):
                    l = QKV_LAYER[what]
                    t, m = (n // 2, n % 2) if kind == "Q" else (n, 2)
                    tok, cols = slice(P * t, P * (t + 1)), slice(INNER * m, INNER * (m + 1))
                    last = split_matmul(bank[:], hi[:, tok], lo[:, tok], wqkv_hi[:, l, cols], wqkv_lo[:, l, cols], True)
                if kind == "VALF":
                    tok = slice(P * n, P * (n + 1))
                    last = split_matmul(bank[:], hi[:, tok], lo[:, tok], wf_hi[:, 2], wf_lo[:, 2], True)
                if kind == "QF":
                    for m in range(2):
                        c = 2 * (n % 2) + m
                        cols = slice(P * c, P * (c + 1))
                        last = split_matmul(bank[:, T * m:T * (m + 1)], hi[:], lo[:], wf_hi[:, n // 2, cols],
                                            wf_lo[:, n // 2, cols], False)
                if kind == "R":
                    pe.wait_ge(sems["rope_ready"], count(i, "rope_ready", ("Q",) + step[1:]))
                    u = ROPE_NO[("Q",) + step[1:]] % ROPES
                    for c in range(CHUNKS):
                        last = nc.tensor.transpose(bank[:, P * c:P * (c + 1)], roped[:, u, P * c:P * (c + 1)], ident[:])
                last.then_inc(sems["bank_filled"], 1)

            with pe.Fori(0, ITERS) as i:
                for step in ORDER:
                    if step[0] == "S":
                        scores(i, step)
                    elif step[0] == "T":
                        turn(i, step)
                    elif step[0] == "V":
                        values(i, step)
                    elif step[0] in DENSE:
                        dense(i, step)
                pe.wait_ge(sems["x_ready"], count(i, "x_ready", LAST))


_INS = ["L0_attn_x", "L0_attn_Wq", "L0_attn_bq", "L0_attn_Wk", "L0_attn_bk", "L0_attn_Wv", "L0_attn_bv", "L0_attn_Wo",
        "L0_attn_bo", "L0_ffn_wqkv", "L0_ffn_q_scale", "L0_ffn_k_scale", "L0_ffn_wo", "L0_ffn_ln_g", "L0_ffn_ln_b",
        "L0_ffn_w1", "L0_ffn_b1", "L0_ffn_w2", "L0_ffn_b2"]


def rope_table():
    half = np.arange(0, LOCAL_D, 2, dtype=np.float64)
    freqs = np.arange(T)[:, None] * (1.0 / 10000.0 ** (half / LOCAL_D))[None, :].astype(np.float32)
    freqs = np.concatenate([freqs, freqs], -1)
    base = (half + 0.4 * LOCAL_D) / (1.4 * LOCAL_D)
    power = (np.arange(T) - T // 2) / (WINDOW // 2)
    scale = base[None, :] ** power[:, None]
    scale = np.concatenate([scale, scale], -1)
    sign = np.where(np.arange(LOCAL_D) < LOCAL_D // 2, -1.0, 1.0)
    table = np.zeros((T, 2, 2, LOCAL_D))
    for m, s in enumerate((8.0 * scale, 1.0 / scale)):
        table[:, 0, m] = np.cos(freqs) * s
        table[:, 1, m] = np.sin(freqs) * sign * s
    return table.astype(np.float32)


def kernel(**inputs):
    import concourse.bacc as bacc
    from concourse.bass_utils import run_bass_kernel_spmd

    nc = bacc.Bacc("TRN2", target_bir_lowering=False, num_devices=1)
    arrays, args = {}, {}
    for name in _INS + ["rope"]:
        x = rope_table() if name == "rope" else np.ascontiguousarray(inputs[name])
        arrays[f"in_{name}_dram"] = x
        args[name] = nc.dram_tensor(f"in_{name}_dram", x.shape, mybir.dt.from_np(x.dtype), kind="ExternalInput").ap()
    out = nc.dram_tensor("out_0_dram", (SEQS, T, C), F32, kind="ExternalOutput").ap()
    macaron(nc, args, out)
    r = run_bass_kernel_spmd(nc, [arrays], core_ids=[0])
    return r.results[0]["out_0_dram"]
```

```python
from contextlib import ExitStack

import numpy as np

import concourse.bass as bass
from concourse import mybir

F32 = mybir.dt.float32
F32R = mybir.dt.float32r
BF16 = mybir.dt.bfloat16
ALU = mybir.AluOpType
ACT = mybir.ActivationFunctionType
AX = mybir.AxisListType.X
AXY = mybir.AxisListType.XY

P = 128
SEQS, T, C = 16, 256, 128
TILES = T // P
STREAMS = 4
LAYERS = 2
LOCAL_HEADS, LOCAL_D = 8, 64
WINDOW = 64
INNER = LOCAL_HEADS * LOCAL_D
HID = int(C * 4 * 2 / 3)
FULL_HEADS, FULL_D = 16, 8
PAD_D = 32
CHUNKS = INNER // P
HALF = C // 2
HID_ROWS = [min(P, HID - P * n) for n in range((HID + P - 1) // P)]
HC = len(HID_ROWS)
EPS = 1e-5
NORM_FLOOR = 1e-12
MASKED = -1e30
LOCAL_KEY0 = P - WINDOW
LOCAL_COLS = P + T - LOCAL_KEY0
FULL_COLS = P + T
STACKED = (0, 1, 2)
LOW_BLOCK = (1, 2)
FULL_SCALE = float(np.float32(1.0) / np.sqrt(np.float32(FULL_D)))
DENSE_BANKS = 3
SCORE_BANKS = 2
PROBS = 4
TURNED = 6
ROPES = 2

PHASES = [("D", "enter"), ("A", 0), ("D", "mid"), ("A", 1), ("D", "to_full"), ("A", "full"),
          ("D", "from_full"), ("A", 0), ("D", "mid"), ("A", 1), ("D", "leave")]
DENSE_LAYER = {"mid": 0, "to_full": 1, "leave": 1}
QKV_LAYER = {"enter": 0, "mid": 1, "from_full": 0}


def heads_of(phase):
    return FULL_HEADS if PHASES[phase][1] == "full" else LOCAL_HEADS


def is_full(phase):
    return PHASES[phase][1] == "full"


def dense_parts(s, ph):
    what = PHASES[ph][1]
    front, back = [], []
    if what == "enter":
        front += [("COPY", s, ph, 0)]
    if what in DENSE_LAYER:
        front += [("WO", s, ph, 0), ("LNH", s, ph, 0), ("NORM", s, ph, 0), ("LNT", s, ph, 0)]
        front += [("W1", s, ph, n) for n in range(HC)] + [("W2", s, ph, 0)]
    if what == "from_full":
        front += [("WOF", s, ph, 0)]
    if what in ("to_full", "from_full", "leave"):
        front += [("XADD", s, ph, 0)]
    if what in ("enter", "to_full", "from_full"):
        front += [("LNX", s, ph, 0), ("NORM", s, ph, 1)]
    if what in ("enter", "from_full"):
        front += [("STATE", s, ph, 0)]
    if what in QKV_LAYER:
        front += [("SPLIT", s, ph, 0)]
        back += [("Q", s, ph, 0), ("Q", s, ph, 1), ("VAL", s, ph, 0), ("Q", s, ph, 2), ("R", s, ph, 0),
                 ("Q", s, ph, 3), ("R", s, ph, 1), ("VAL", s, ph, 1), ("R", s, ph, 2), ("R", s, ph, 3)]
    if what == "to_full":
        front += [("LNT", s, ph, 1)]
        back += [("QF", s, ph, n) for n in range(4)] + [("VALF", s, ph, n) for n in range(TILES)]
    return front, back


def group_done(step):
    return not is_full(step[2]) or step[3] % 2 == 1


DENSE = {"WO", "LNH", "LNT", "W1", "W2", "WOF", "XADD", "STATE", "Q", "VAL", "R", "QF", "VALF"}
PE, ACTE, DVE, POOL = range(4)
PASSES = {
    "N": [(DVE, 0.64)], "T": [(PE, 0.35), (ACTE, 0.48)], "COPY": [(DVE, 0.2)], "SPLIT": [(DVE, 0.66)],
    "WO": [(PE, 1.9), (DVE, 0.67)], "LNH": [(PE, 0.22), (DVE, 0.9), (POOL, 0.2)], "LNX": [(DVE, 0.9), (POOL, 0.2)],
    "NORM": [(DVE, 0.66)], "LNT": [(PE, 0.22), (ACTE, 0.45), (DVE, 0.35)], "STATE": [(PE, 0.22), (ACTE, 0.85)],
    "W1": [(PE, 0.75), (ACTE, 0.45), (DVE, 0.4)], "W2": [(PE, 1.5), (DVE, 0.8)], "WOF": [(PE, 1.8), (DVE, 0.4)],
    "XADD": [(PE, 0.22), (DVE, 0.35)], "Q": [(PE, 0.7), (ACTE, 0.65), (DVE, 1.85), (POOL, 3.1)],
    "VAL": [(PE, 0.7), (ACTE, 0.65)], "VALF": [(PE, 0.7), (ACTE, 0.65)], "R": [(PE, 0.47), (ACTE, 0.65)],
    "QF": [(PE, 0.7), (ACTE, 1.1), (DVE, 0.75)]}
HANDOVER = 0.2
TABLE_CHANGE = 1.3
FRONT_AT, BACK_AT = 2.0, 10.0
URGENT = {"LNH": 4.0, "NORM": 4.0, "LNT": 4.0, "W1": 4.0, "W2": 4.0, "XADD": 4.0, "WO": 4.0, "WOF": 4.0, "SPLIT": 4.0,
          "STATE": 4.0, "LNX": 4.0}


def passes(step):
    kind, _, ph, _ = step
    if kind == "S":
        return [(PE, 0.6), (DVE, 0.55), (ACTE, 0.75)] if is_full(ph) else [(PE, 0.75), (DVE, 0.47), (ACTE, 0.72)]
    if kind == "V":
        return [(PE, 0.5 if is_full(ph) else 0.65)] + ([(ACTE, 0.45)] if group_done(step) else [])
    return PASSES[kind]


def schedule():
    turns = [(s, ph) for ph in range(1, len(PHASES), 2) for s in range(STREAMS)]
    first = {}
    at = 0
    for turn in turns:
        first[turn] = at
        at += heads_of(turn[1])
    age, lines = {}, {"S": [], "N": [], "T": [], "V": [], "front": [], "back": []}
    for s, ph in turns:
        for h in range(heads_of(ph)):
            r = first[s, ph] + h
            for kind, n, later in (("S", h, 0.0), ("N", h, 0.5), ("T", h, 1.5)) + ((("V", h // 2, 2.5),) if h % 2 else ()):
                age[kind, s, ph, n] = r + later
                lines[kind].append((kind, s, ph, n))
    parts = []
    for s in range(STREAMS):
        for ph in range(0, len(PHASES), 2):
            start = first[s, ph - 1] + heads_of(ph - 1) if ph else first[s, 1] - 2 * LOCAL_HEADS
            front, back = dense_parts(s, ph)
            parts.append((start, front, back))
    parts.sort(key=lambda x: (x[0], x[1][0][2]))
    after = {}

    def wait(step, part, other, other_part=-1):
        after.setdefault((step, part), []).append((other, other_part % len(passes(other))))

    for start, front, back in parts:
        lines["front"] += front
        lines["back"] += back
        for n, x in enumerate(front):
            age[x] = start + FRONT_AT + 0.3 * n
            if n and x[0] != "W1":
                wait(x, 0, front[n - 1])
            elif n:
                wait(x, 0, [y for y in front if y[0] == "LNT"][0])
        for n, x in enumerate(back):
            age[x] = start + BACK_AT + 0.3 * n
            wait(x, 0, front[-1])
            if x[0] == "R":
                wait(x, 0, ("Q",) + x[1:])
        s, ph = front[0][1:3]
        if ph:
            wait(front[0], 0, ("V", s, ph - 1, heads_of(ph - 1) // 2 - 1))
        if ph + 1 < len(PHASES):
            for x in back:
                wait(("S", s, ph + 1, 0), 0, x)
        gates = [x for x in front if x[0] == "W1"]
        if gates:
            wait(gates[0], 1, gates[-1], 0)
            for x, y in zip(gates[1:], gates):
                wait(x, 1, y, 1)
    for odd in (0, 1):
        mine = [(f, b) for _, f, b in parts if f[0][1] % 2 == odd]
        for (_, b), (f, _) in zip(mine, mine[1:]):
            for x in f:
                if x[0] in ("LNT", "STATE") and b:
                    wait(x, 0, b[-1])
    heads = lines["S"]
    for g, x in enumerate(heads):
        _, s, ph, h = x
        wait(("N",) + x[1:], 0, x)
        wait(("T",) + x[1:], 0, ("N",) + x[1:])
        if g >= SCORE_BANKS:
            wait(x, 0, heads[g - SCORE_BANKS])
        if g >= 2:
            wait(("T",) + x[1:], 0, ("T",) + heads[g - 2][1:])
        if g >= PROBS:
            wait(x, 2, ("T",) + heads[g - PROBS][1:], 0)
        if g >= TURNED:
            before = heads[g - TURNED]
            wait(("T",) + x[1:], 1, ("V",) + before[1:3] + (before[3] // 2,), 0)
    last_v = None
    for x in lines["V"]:
        wait(x, 0, ("T",) + x[1:3] + (2 * x[3] + 1,))
        if last_v is not None and (not is_full(x[2]) or x[3] % 2 == 0):
            wait(x, 0, last_v)
        if group_done(x):
            last_v = x
    ropes = [x for x in lines["back"] if x[0] == "Q"]
    for u, x in enumerate(ropes[ROPES:]):
        wait(x, 3, ("R",) + ropes[u][1:], 0)
        wait(x, 2, ropes[u])
        wait(x, 1, ropes[u], 2)

    waiting = [[] for _ in range(4)]
    for line in lines.values():
        for n, x in enumerate(line):
            for part, (engine, _) in enumerate(passes(x)):
                if part:
                    wait(x, part, x, part - 1)
                elif n:
                    wait(x, 0, line[n - 1], 0)
                waiting[engine].append((age[x] - (URGENT.get(x[0], 0.0) if engine != PE else 0.0), x, part))
    for w in waiting:
        w.sort(key=lambda y: y[0])
    done, free, orders, started = {}, [0.0] * 4, [[], [], [], []], {}
    filled, held, gelu_next = [], None, None
    while any(waiting):
        best = None
        for engine in range(4):
            choice = None
            for entry in waiting[engine][:400]:
                _, x, part = entry
                ready = 0.0
                if engine == PE and x[0] in DENSE:
                    if held is not None and x != held:
                        continue
                    if len(filled) >= DENSE_BANKS:
                        before = filled[-DENSE_BANKS]
                        if before[0] == "LNH":
                            before = ("NORM",) + before[1:]
                        release = (before, 2 if before[0] == "Q" else len(passes(before)) - 1)
                        if release not in done:
                            continue
                        ready = done[release] + HANDOVER
                if engine == ACTE and gelu_next is not None and x != gelu_next:
                    continue
                for b in after.get((x, part), ()):
                    if b not in done:
                        ready = None
                        break
                    ready = max(ready, done[b] + (HANDOVER if passes(b[0])[b[1]][0] != engine else 0.0))
                if ready is None:
                    continue
                start = max(ready, free[engine])
                if choice is None or start < choice[0] - 1e-9:
                    choice = (start, entry)
                if ready <= free[engine]:
                    break
            if choice is not None and (best is None or choice[0] < best[0]):
                best = (choice[0], engine, choice[1])
        start, engine, entry = best
        _, x, part = entry
        waiting[engine].remove(entry)
        lasts = passes(x)[part][1]
        if x[0] == "W1":
            more = x[:3] + (x[3] + 1,) if x[3] + 1 < HC else None
            if engine == PE:
                held = more
            if engine == ACTE:
                lasts += TABLE_CHANGE if x[3] in (0, HC - 1) else 0.0
                gelu_next = more
        if engine == PE and x[0] in DENSE:
            filled.append(x)
        done[x, part] = free[engine] = start + lasts
        if x not in started:
            started[x] = start
        orders[engine].append(x)
    order = sorted(started, key=lambda x: started[x])
    return [order] + orders


ORDER, PE_ORDER, ACT_ORDER, DVE_ORDER, POOL_ORDER = schedule()


def last_step(kinds, step):
    here = ORDER.index(step)
    for x in reversed(ORDER[:here]):
        if x[0] in kinds and x[1] == step[1]:
            return x
    raise ValueError(step)


def numbered(kinds):
    return {step: n for n, step in enumerate(x for x in PE_ORDER if x[0] in kinds)}


HEAD_NO = numbered({"S"})
DENSE_NO = numbered(DENSE)
ROPE_NO = numbered({"Q"})
HEAD_AT = {n: step for step, n in HEAD_NO.items()}
DENSE_AT = {n: step for step, n in DENSE_NO.items()}
ROPE_AT = {n: step for step, n in ROPE_NO.items()}


def emits(step):
    kind = step[0]
    out = {
        "S": {"scores_ready": 1, "max_ready": 1, "probs_ready": 1},
        "N": {"vector_step": 1, "probs_scaled": 1},
        "T": {"probs_turned": 1, "turned_copied": 1},
        "V": {"heads_summed": 1, "heads_copied": int(kind == "V" and group_done(step))},
        "COPY": {"x_taken": 1},
        "WO": {"state_ready": 1},
        "LNH": {"vector_step": 2, "var_ready": 1, "rstd_ready": 1},
        "LNX": {"vector_step": 2, "var_ready": 1, "rstd_ready": 1},
        "NORM": {"normed": 1},
        "LNT": {"high_ready": 1, "split_ready": 1},
        "W1": {"gelu_ready": 1, "hidden_ready": 1},
        "W2": {"state_ready": 1},
        "WOF": {"state_ready": 1},
        "XADD": {"x_ready": 1},
        "STATE": {"state_set": 1},
        "SPLIT": {"vector_step": 1, "split_ready": 1},
        "Q": {"squares_ready": 1, "squares_summed": 1, "rope_parts": 1, "vector_step": 1, "pool_step": 2, "rope_ready": 1},
        "VAL": {"values_ready": 1},
        "VALF": {"values_ready": 1},
        "R": {"qk_ready": 1},
        "QF": {"high_parts": 1, "stacked": 1},
    }[kind].copy()
    if kind in DENSE:
        out["bank_filled"] = 1
    return out


RELEASES = {"WO": "state_ready", "NORM": "normed", "LNT": "split_ready", "W1": "hidden_ready",
            "W2": "state_ready", "WOF": "state_ready", "XADD": "x_ready", "STATE": "state_set",
            "Q": "rope_parts", "VAL": "values_ready", "VALF": "values_ready", "R": "qk_ready",
            "QF": "stacked"}


ORDERS = ((PE_ORDER, ("scores_ready", "probs_turned", "heads_summed", "bank_filled")),
          (ACT_ORDER, ("probs_ready", "turned_copied", "heads_copied", "state_set", "high_ready", "squares_ready",
                       "values_ready", "qk_ready", "gelu_ready",
                       "high_parts")),
          (DVE_ORDER, ("max_ready", "vector_step", "probs_scaled", "x_taken", "state_ready", "var_ready", "normed",
                       "split_ready", "hidden_ready", "x_ready", "squares_summed", "rope_parts", "stacked")),
          (POOL_ORDER, ("rstd_ready", "pool_step", "rope_ready")))


def tally():
    total, nth = {}, {}
    for order, names in ORDERS:
        for step in order:
            for name, n in emits(step).items():
                if name in names and n:
                    total[name] = total.get(name, 0) + n
                    nth.setdefault(name, {})[step] = total[name]
    return total, nth


TOTAL, NTH = tally()


V_BEFORE = {}
for _step in ORDER:
    if _step[0] == "V":
        V_BEFORE[_step] = next((x for x in reversed(ORDER[:ORDER.index(_step)]) if x[0] == "V" and group_done(x)), None)
LAST = [x for x in DVE_ORDER if x[0] == "XADD"][-1]


def head_no(step):
    return HEAD_NO[("S",) + step[1:]]


def macaron(nc: bass.Bass, a, out):
    with ExitStack() as ctx:
        def sb(name, shape, dt=F32):
            return ctx.enter_context(nc.sbuf_tensor(name, shape, dt))

        def psum(name):
            return ctx.enter_context(nc.psum_tensor(name, [P, 512], F32))

        def sem(name):
            return ctx.enter_context(nc.semaphore(name))

        wqkv_hi = sb("wqkv_hi", [P, LAYERS, 3 * INNER], F32R)
        wqkv_lo = sb("wqkv_lo", [P, LAYERS, 3 * INNER], F32R)
        w1_hi = sb("w1_hi", [P, LAYERS, 2 * HID], F32R)
        w1_lo = sb("w1_lo", [P, LAYERS, 2 * HID], F32R)
        wf_hi = sb("wf_hi", [P, 3, FULL_HEADS * PAD_D], F32R)
        wf_lo = sb("wf_lo", [P, 3, FULL_HEADS * PAD_D], F32R)
        wo = sb("wo", [P, LAYERS, CHUNKS, C])
        w2 = sb("w2", [P, LAYERS, HC, C])
        wof = sb("wof", [P, CHUNKS, C])
        lng = sb("lng", [P, LAYERS])
        lnb = sb("lnb", [P, LAYERS])
        b1 = sb("b1", [P, LAYERS, 2 * HC])
        b1f = sb("b1f", [P, LAYERS, 2 * HC])
        b2 = sb("b2", [P, LAYERS])
        bof = sb("bof", [P, 1])
        biasf = sb("biasf", [P, 3, CHUNKS])
        low_rows = sb("low_rows", [P, 2])
        low_bias = sb("low_bias", [P, 2, CHUNKS])
        rope = sb("rope", [P, LAYERS, TILES, 2, 2, LOCAL_D])
        ident = sb("ident", [P, P])
        ident_b = sb("ident_b", [P, P], BF16)
        mask_local = sb("mask_local", [P, LOCAL_COLS], BF16)
        mask_full = sb("mask_full", [P, FULL_COLS], BF16)
        neg_half = sb("neg_half", [P, LOCAL_HEADS])
        neg_max = sb("neg_max", [P, PROBS, TILES])
        prob_sum = sb("prob_sum", [P, PROBS, TILES])
        prob_inv = sb("prob_inv", [P, PROBS, TILES])
        probs_local = sb("probs_local", [P, PROBS, P + T])

        def per_stream(name, shape, dt=F32):
            return [sb(f"{name}{s}", shape, dt) for s in range(STREAMS)]

        x_in = per_stream("x_in", [P, TILES, C])
        x_sb = per_stream("x_sb", [P, TILES, C])
        state = per_stream("state", [P, T + 1])
        y_t = per_stream("y_t", [P, T])

        with ExitStack() as setup:
            def staged(name, shape):
                return setup.enter_context(nc.sbuf_tensor(name, shape, F32))

            stage = staged("stage", [P, LAYERS, 3 * INNER])
            stage1 = staged("stage1", [P, LAYERS, 2 * HID])
            scaled1 = staged("scaled1", [P, LAYERS, 2 * HID])
            stagef = staged("stagef", [P, 3, C])
            padded = staged("padded", [P, 3, FULL_HEADS, PAD_D])
            rope_in = staged("rope_in", [P, TILES, 2, 2, LOCAL_D])
            qk_scale = staged("qk_scale", [P, 2, LAYERS, LOCAL_D])

        with ExitStack() as place:
            stacked_q, stacked_k = ([place.enter_context(nc.sbuf_tensor(f"stacked_{m}{s}", [P, CHUNKS, T], F32R))
                                     for s in range(STREAMS)] for m in "qk")
        q_t = per_stream("q_t", [P, CHUNKS, T])
        o_t = q_t
        k_t = per_stream("k_t", [P, CHUNKS, T])
        normal = per_stream("normal", [P, TILES, C])
        bn = per_stream("bn", [P, TILES, 6])
        mean_var = per_stream("mean_var", [P, TILES, 2])
        var_eps = per_stream("var_eps", [P, TILES])
        rstd = per_stream("rstd", [P, TILES])
        val = per_stream("val", [P, TILES, INNER])

        h_hi = [sb(f"h_hi{n}", [P, T], F32R) for n in range(2)] * (STREAMS // 2)
        h_lo = [sb(f"h_lo{n}", [P, T], F32R) for n in range(2)] * (STREAMS // 2)
        gelu = sb("gelu", [P, HC, T])
        hidden = sb("hidden", [P, HC, T])
        high = sb("high", [P, 2, T], F32R)
        squares = sb("squares", [P, ROPES, INNER])
        sums = sb("sums", [P, ROPES, LOCAL_HEADS])
        sums_floor = sb("sums_floor", [P, ROPES, LOCAL_HEADS])
        rnorm = sb("rnorm", [P, ROPES, LOCAL_HEADS])
        parts = sb("parts", [P, ROPES, 2, INNER])
        roped = sb("roped", [P, ROPES, INNER])
        probs_full = sb("probs_full", [P, PROBS, P + T])
        turned = sb("turned", [P, TURNED, P + T])

        ps_scores = [psum(f"ps_scores{n}") for n in range(SCORE_BANKS)]
        ps_turned = [psum(f"ps_turned{n}") for n in range(2)]
        ps_heads = psum("ps_heads")
        ps_dense = [psum(f"ps_dense{n}") for n in range(DENSE_BANKS)]

        w_loaded = sem("w_loaded")
        f_loaded = sem("f_loaded")
        x_loaded = [sem(f"x_loaded{s}") for s in range(STREAMS)]
        stored = [sem(f"stored{s}") for s in range(STREAMS)]
        cleared = sem("cleared")
        pads_cleared = sem("pads_cleared")
        fold_summed = sem("fold_summed")
        setup_step = sem("setup_step")
        weights_ready = sem("weights_ready")
        sems = {name: sem(name) for name in TOTAL}

        def count(i, name, step, back=0):
            return i * TOTAL[name] + (NTH[name][step] - back)

        block = ctx.enter_context(nc.Block())

        x_dram = a["L0_attn_x"].rearrange("(n s) (t p) c -> n s p t c", s=STREAMS, p=P)
        out_dram = out.rearrange("(n s) (t p) c -> n s p t c", s=STREAMS, p=P)
        ITERS = SEQS // STREAMS
        N_WLOADS = 1 + 2 * LAYERS + 3 + LAYERS * (3 + 2 * HC) + 4
        N_FLOADS = (2 * len(STACKED) + 2) * P // PAD_D
        N_SELECTS = 8

        def w1_cols(n):
            at = P * (n % HC) + (HID if n >= HC else 0)
            return at, HID_ROWS[n % HC]

        @block.sync
        def _(sp):
            def load_x(n, s):
                sp.dma_start(x_in[s][:], x_dram[n, s]).then_inc(x_loaded[s], 16)

            for s in range(STREAMS):
                load_x(0, s)
            n = 0

            def load(dst, src):
                sp.dma_start(dst, src).then_inc(w_loaded, 16)
                return 1

            with nc.allow_non_contiguous_dma(reason="bias columns, once"):
                n += load(rope_in[:], a["rope"].rearrange("(t p) a b d -> p t a b d", p=P))
                for m, name in enumerate(("L0_ffn_q_scale", "L0_ffn_k_scale")):
                    for l in range(LAYERS):
                        src = a[name][l:l + 1].to_broadcast([P, LOCAL_D])
                        sp.dma_start(qk_scale[:, m, l], src).then_inc(stored[2 * m + l], 16)
                for l in range(LAYERS):
                    n += load(stage[:, l], a["L0_ffn_wqkv"][l])
                    n += load(stage1[:, l], a["L0_ffn_w1"][l])
                for m, w in enumerate(("L0_attn_Wq", "L0_attn_Wk", "L0_attn_Wv")):
                    n += load(stagef[:, m], a[w])
                for l in range(LAYERS):
                    n += load(wo[:, l], a["L0_ffn_wo"][l].rearrange("(c p) n -> p c n", p=P))
                    full = HID // P
                    n += load(w2[:, l, 0:full], a["L0_ffn_w2"][l, 0:full * P].rearrange("(c p) n -> p c n", p=P))
                    n += load(w2[0:HID_ROWS[-1], l, full], a["L0_ffn_w2"][l, full * P:HID])
                    for m in range(2 * HC):
                        at, rows = w1_cols(m)
                        n += load(b1[0:rows, l, m:m + 1], a["L0_ffn_b1"][l, at:at + rows].rearrange("(p o) -> p o", o=1))
                for dst, src in ((lng, "L0_ffn_ln_g"), (lnb, "L0_ffn_ln_b"), (b2, "L0_ffn_b2")):
                    n += load(dst[:], a[src].rearrange("l p -> p l"))
                n += load(bof[:], a["L0_attn_bo"].rearrange("(p o) -> p o", o=1))
                assert n == N_WLOADS, n
                sp.wait_ge(pads_cleared, 1)
                m = 0
                for j in range(P // PAD_D):
                    rows = slice(PAD_D * j, PAD_D * j + FULL_D)
                    for b, name in enumerate(("L0_attn_bq", "L0_attn_bk", "L0_attn_bv")):
                        for part in STACKED if b < 2 else (0,):
                            at = PAD_D * j + FULL_D * part
                            sp.dma_start(biasf[at:at + FULL_D, b, :], a[name].rearrange("(c j d) -> j d c", j=4, d=FULL_D)[j]).then_inc(f_loaded, 16)
                            m += 1
                    sp.dma_start(wof[rows], a["L0_attn_Wo"].rearrange("(c j d) n -> j d c n", j=4, d=FULL_D)[j]).then_inc(f_loaded, 16)
                    m += 1
                assert m == N_FLOADS

            def store(i, s):
                sp.wait_ge(sems["x_ready"], count(i, "x_ready", ("XADD", s, len(PHASES) - 1, 0)))
                sp.dma_start(out_dram[i, s], x_sb[s][:]).then_inc(stored[s], 16)

            with sp.Fori(0, ITERS - 1) as i:
                for s in range(STREAMS):
                    sp.wait_ge(sems["x_taken"], count(i, "x_taken", ("COPY", s, 0, 0)))
                    load_x(i + 1, s)
                for s in range(STREAMS):
                    store(i, s)
            for s in range(STREAMS):
                store(ITERS - 1, s)
            for s in range(STREAMS):
                sp.wait_ge(stored[s], 16 * (ITERS + 1))

        @block.gpsimd
        def _(pool):
            nc.gpsimd.memset(padded[:], 0.0)
            nc.gpsimd.memset(biasf[:], 0.0)
            nc.gpsimd.memset(wof[:], 0.0).then_inc(pads_cleared, 1)
            nc.gpsimd.memset(ident[:], 0.0)
            nc.gpsimd.memset(ident_b[:], 0.0)
            nc.gpsimd.memset(mask_local[:], 0.0)
            nc.gpsimd.memset(mask_full[:], 0.0)
            nc.gpsimd.memset(neg_half[:], -0.5)
            nc.gpsimd.memset(probs_local[:], 0.0).then_inc(cleared, 1)
            pool.wait_ge(cleared, 1)
            n = 1

            def select(t, base, step, chan, op, fill):
                nonlocal n
                nc.gpsimd.affine_select(out=t, in_=t, compare_op=op, fill=fill, base=base,
                                        pattern=[[step, t.shape[1]]], channel_multiplier=chan).then_inc(cleared, 1)
                n += 1
                pool.wait_ge(cleared, n)

            select(ident[:], 0, -1, 1, ALU.not_equal, 1.0)
            select(ident_b[:], 0, -1, 1, ALU.not_equal, 1.0)
            select(mask_local[:, 0:P], 0, -1, 1, ALU.is_ge, MASKED)
            select(mask_local[:, 0:P], WINDOW, 1, -1, ALU.is_ge, MASKED)
            select(mask_local[:, P:], 0, 1, -1, ALU.is_ge, MASKED)
            select(mask_local[:, P:], WINDOW, -1, 1, ALU.is_ge, MASKED)
            select(mask_full[:, 0:P], 0, -1, 1, ALU.is_ge, MASKED)
            select(mask_full[:, P:], P, -1, 1, ALU.is_ge, MASKED)
            assert n == 1 + N_SELECTS

            def norm_scale(i, step):
                s = step[1]
                pool.wait_ge(sems["var_ready"], count(i, "var_ready", step))
                nc.gpsimd.tensor_tensor(rstd[s][:], var_eps[s][:], neg_half[:, 0:TILES], ALU.pow).then_inc(sems["rstd_ready"], 1)

            def rope_join(i, step):
                u = ROPE_NO[step] % ROPES
                pool.wait_ge(sems["rope_parts"], count(i, "rope_parts", step))
                joined = parts[:, u, 0].rearrange("p (h d) -> p h d", d=LOCAL_D)
                sines = parts[:, u, 1].rearrange("p (h d) -> p h d", d=LOCAL_D)
                hd = LOCAL_D // 2
                for half in range(2):
                    dst, src = slice(hd * half, hd * (half + 1)), slice(hd * (1 - half), hd * (2 - half))
                    last = nc.gpsimd.tensor_tensor(joined[:, :, dst], joined[:, :, dst], sines[:, :, src], ALU.add)
                last.then_inc(sems["pool_step"], 1)
                pool.wait_ge(sems["squares_summed"], count(i, "squares_summed", step))
                nc.gpsimd.tensor_tensor(rnorm[:, u], sums_floor[:, u], neg_half[:], ALU.pow).then_inc(sems["pool_step"], 1)
                if ROPE_NO[step] >= ROPES:
                    before = ROPE_AT[ROPE_NO[step] - ROPES]
                    pool.wait_ge(sems["bank_filled"], count(i, "bank_filled", ("R",) + before[1:]))
                pool.wait_ge(sems["pool_step"], count(i, "pool_step", step))
                nc.gpsimd.tensor_tensor(roped[:, u].rearrange("p (h d) -> p h d", d=LOCAL_D),
                                        joined,
                                        rnorm[:, u].rearrange("p (h o) -> p h o", o=1).to_broadcast([P, LOCAL_HEADS, LOCAL_D]),
                                        ALU.mult).then_inc(sems["rope_ready"], 1)

            with pool.Fori(0, ITERS) as i:
                for step in POOL_ORDER:
                    if step[0] == "Q":
                        rope_join(i, step)
                    else:
                        norm_scale(i, step)
                pool.wait_ge(sems["x_ready"], count(i, "x_ready", LAST))

        @block.scalar
        def _(act):
            def exp_scores(i, step):
                s, ph = step[1:3]
                g = HEAD_NO[step]
                u, bank = g % PROBS, ps_scores[g % SCORE_BANKS]
                act.wait_ge(sems["max_ready"], count(i, "max_ready", step))
                if g >= PROBS:
                    act.wait_ge(sems["probs_turned"], count(i, "probs_turned", ("T",) + HEAD_AT[g - PROBS][1:]))
                probs, at = (probs_full, P) if is_full(ph) else (probs_local, P + LOCAL_KEY0)
                cols = FULL_COLS if is_full(ph) else LOCAL_COLS
                for t, (dst, src) in enumerate(((probs[:, u, 0:P], bank[:, 0:P]),
                                                (probs[:, u, at:P + T], bank[:, P:cols]))):
                    last = nc.scalar.activation(dst, src, ACT.Exp, bias=neg_max[:, u, t:t + 1],
                                                accum_out=prob_sum[:, u, t:t + 1])
                last.then_inc(sems["probs_ready"], 1)

            def copy_turned(i, step):
                g = head_no(step)
                act.wait_ge(sems["probs_turned"], count(i, "probs_turned", step))
                if g >= TURNED:
                    h = HEAD_AT[g - TURNED]
                    act.wait_ge(sems["heads_summed"], count(i, "heads_summed", ("V", h[1], h[2], h[3] // 2)))
                cols = FULL_COLS if is_full(step[2]) else LOCAL_COLS
                nc.scalar.activation(turned[:, g % TURNED, 0:cols], ps_turned[g % 2][:, 0:cols],
                                     ACT.Copy).then_inc(sems["turned_copied"], 1)

            def copy_heads(i, step):
                s, ph, n = step[1:]
                act.wait_ge(sems["heads_summed"], count(i, "heads_summed", step))
                if is_full(ph):
                    c = n // 2
                    nc.scalar.activation(o_t[s][:, c], ps_heads[:, 0:T], ACT.Identity,
                                         bias=biasf[:, 2, c:c + 1]).then_inc(sems["heads_copied"], 1)
                else:
                    nc.scalar.activation(o_t[s][:, n], ps_heads[:, 0:T], ACT.Copy).then_inc(sems["heads_copied"], 1)

            def dense(i, step):
                kind, s, ph, n = step
                bank = ps_dense[DENSE_NO[step] % DENSE_BANKS]
                act.wait_ge(sems["bank_filled"], count(i, "bank_filled", step))
                if kind == "STATE":
                    nc.scalar.activation(state[s][0:HALF, 0:T], bank[0:HALF, 0:T], ACT.Copy)
                    nc.scalar.activation(state[s][HALF:C, 1:T + 1], bank[HALF:C, 0:T], ACT.Copy).then_inc(sems["state_set"], 1)
                if kind == "LNT":
                    nc.scalar.activation(h_hi[s][:], bank[:, 0:T], ACT.Copy).then_inc(sems["high_ready"], 1)
                if kind == "Q":
                    u = ROPE_NO[step]
                    if u >= ROPES:
                        act.wait_ge(sems["squares_summed"], count(i, "squares_summed", ROPE_AT[u - ROPES]))
                    nc.scalar.activation(squares[:, u % ROPES], bank[:], ACT.Square).then_inc(sems["squares_ready"], 1)
                if kind in ("VAL", "VALF"):
                    nc.scalar.activation(val[s][:, n], bank[:], ACT.Copy).then_inc(sems["values_ready"], 1)
                if kind == "R":
                    dst = (q_t if n % 2 == 0 else k_t)[s]
                    nc.scalar.activation(dst[:, :, P * (n // 2):P * (n // 2 + 1)],
                                         bank[:].rearrange("p (c q) -> p c q", c=CHUNKS), ACT.Copy).then_inc(sems["qk_ready"], 1)
                if kind == "QF":
                    if n > 0:
                        act.wait_ge(sems["stacked"], count(i, "stacked", ("QF", s, ph, n - 1)))
                    w = n // 2
                    for m in range(2):
                        c = 2 * (n % 2) + m
                        last = nc.scalar.activation(high[:, m], bank[:, T * m:T * (m + 1)], ACT.Identity,
                                                    bias=low_bias[:, w, c:c + 1], scale=low_rows[:, w:w + 1])
                    last.then_inc(sems["high_parts"], 1)
                if kind == "W1":
                    l, rows = DENSE_LAYER[PHASES[ph][1]], HID_ROWS[n]
                    nc.scalar.activation(gelu[0:rows, n], bank[0:rows, 0:T], ACT.Gelu,
                                         bias=b1f[0:rows, l, HC + n:HC + n + 1]).then_inc(sems["gelu_ready"], 1)

            act.wait_ge(weights_ready, 1)
            with act.Fori(0, ITERS) as i:
                for step in ACT_ORDER:
                    if step[0] == "S":
                        exp_scores(i, step)
                    elif step[0] == "T":
                        copy_turned(i, step)
                    elif step[0] == "V":
                        copy_heads(i, step)
                    else:
                        dense(i, step)
                act.wait_ge(sems["x_ready"], count(i, "x_ready", LAST))

        @block.vector
        def _(dve):
            links = [0]

            def link(ins):
                links[0] += 1
                ins.then_inc(setup_step, 1)
                dve.wait_ge(setup_step, links[0])

            dve.wait_ge(w_loaded, 16 * N_WLOADS)
            for s in range(STREAMS):
                dve.wait_ge(stored[s], 16)
            dve.wait_ge(pads_cleared, 1)
            for s in range(STREAMS):
                nc.vector.memset(state[s][HALF:C, 0:1], 0.0)
            for l in range(LAYERS):
                nc.vector.tensor_copy(wqkv_hi[:, l], stage[:, l])
                nc.vector.tensor_scalar(scaled1[:, l], stage1[:, l], lng[:, l:l + 1], None, ALU.mult)
                for t in range(TILES):
                    last = nc.vector.tensor_tensor(rope[:, l, t], rope_in[:, t],
                                                   qk_scale[:, :, l].rearrange("p (o m) d -> p o m d", o=1).to_broadcast(
                                                       [P, 2, 2, LOCAL_D]), ALU.mult)
            for m in range(3):
                for part in STACKED if m < 2 else (0,):
                    last = nc.vector.tensor_scalar(padded[:, m, :, FULL_D * part:FULL_D * (part + 1)],
                                                   stagef[:, m].rearrange("p (h d) -> p h d", d=FULL_D),
                                                   FULL_SCALE if m == 0 else 1.0, None, ALU.mult)
            link(last)
            nc.vector.tensor_copy(wf_hi[:], padded[:].rearrange("p m h d -> p m (h d)"))
            link(nc.vector.tensor_copy(w1_hi[:], scaled1[:]))
            for l in range(LAYERS):
                nc.vector.tensor_tensor(wqkv_lo[:, l], stage[:, l], wqkv_hi[:, l].bitcast(F32), ALU.subtract)
            nc.vector.tensor_tensor(w1_lo[:], scaled1[:], w1_hi[:].bitcast(F32), ALU.subtract)
            nc.vector.tensor_tensor(wf_lo[:], padded[:].rearrange("p m h d -> p m (h d)"), wf_hi[:].bitcast(F32), ALU.subtract)
            dve.wait_ge(fold_summed, 1)
            for l in range(LAYERS):
                for m in range(2 * HC):
                    rows = w1_cols(m)[1]
                    nc.vector.tensor_tensor(b1f[0:rows, l, m:m + 1], b1[0:rows, l, m:m + 1],
                                            ps_heads[0:rows, 2 * HC * l + m:2 * HC * l + m + 1], ALU.add)
            dve.wait_ge(f_loaded, 16 * N_FLOADS)
            nc.vector.tensor_scalar(biasf[:, 0], biasf[:, 0], FULL_SCALE, None, ALU.mult)
            dve.wait_ge(cleared, 1 + N_SELECTS)
            for m, block in enumerate(LOW_BLOCK):
                ones = ident[:].rearrange("p (j r) -> p j r", r=PAD_D)[:, :, FULL_D * block:FULL_D * (block + 1)]
                last = nc.vector.tensor_reduce(low_rows[:, m:m + 1], ones, AXY, ALU.add, negate=True)
            link(last)
            for m in range(2):
                last = nc.vector.tensor_scalar(low_bias[:, m], biasf[:, m], low_rows[:, m:m + 1], None, ALU.mult)
            last.then_inc(weights_ready, 1)
            dve.wait_ge(weights_ready, 1)

            def row_max(i, step):
                g = HEAD_NO[step]
                u, bank = g % PROBS, ps_scores[g % SCORE_BANKS]
                cols = FULL_COLS if is_full(step[2]) else LOCAL_COLS
                dve.wait_ge(sems["scores_ready"], count(i, "scores_ready", step))
                nc.vector.tensor_reduce(neg_max[:, u, 0:1], bank[:, 0:P], AX, ALU.max, negate=True)
                nc.vector.tensor_reduce(neg_max[:, u, 1:2], bank[:, P:cols], AX, ALU.max,
                                        negate=True).then_inc(sems["max_ready"], 1)

            def scale_probs(i, step):
                u = head_no(step) % PROBS
                probs, at = (probs_full, P) if is_full(step[2]) else (probs_local, P + LOCAL_KEY0)
                dve.wait_ge(sems["probs_ready"], count(i, "probs_ready", ("S",) + step[1:]))
                nc.vector.reciprocal(prob_inv[:, u], prob_sum[:, u]).then_inc(sems["vector_step"], 1)
                dve.wait_ge(sems["vector_step"], count(i, "vector_step", step))
                nc.vector.tensor_scalar(probs[:, u, 0:P], probs[:, u, 0:P], prob_inv[:, u, 0:1], None, ALU.mult)
                nc.vector.tensor_scalar(probs[:, u, at:P + T], probs[:, u, at:P + T], prob_inv[:, u, 1:2], None,
                                        ALU.mult).then_inc(sems["probs_scaled"], 1)

            def layer_norm(i, step, source):
                s = step[1]
                for t in range(TILES):
                    last = nc.vector.bn_stats(bn[s][:, t], source[t])
                last.then_inc(sems["vector_step"], 1)
                dve.wait_ge(sems["vector_step"], count(i, "vector_step", step, 1))
                nc.vector.memset(var_eps[s][:], 0.0)
                for t in range(TILES):
                    last = nc.vector.bn_aggr(mean_var[s][:, t], bn[s][:, t])
                last.then_inc(sems["vector_step"], 1)
                dve.wait_ge(sems["vector_step"], count(i, "vector_step", step))
                nc.vector.tensor_scalar(var_eps[s][:], mean_var[s][:, :, 1], EPS, None, ALU.add).then_inc(sems["var_ready"], 1)

            def normalise(i, step, source):
                s = step[1]
                dve.wait_ge(sems["rstd_ready"], count(i, "rstd_ready", last_step({"LNH", "LNX"}, step)))
                for t in range(TILES):
                    last = nc.vector.tensor_scalar(normal[s][:, t], source[t], mean_var[s][:, t, 0:1], rstd[s][:, t:t + 1],
                                                   ALU.subtract, ALU.mult)
                last.then_inc(sems["normed"], 1)

            def add_to_state(s, bank, dst, bias):
                for rows, at in ((slice(0, HALF), 0), (slice(HALF, C), 1)):
                    old = state[s][rows, at:at + T]
                    new = dst[rows, :] if dst is not None else old
                    if bias is None:
                        last = nc.vector.tensor_tensor(new, bank[rows, 0:T], old, ALU.add)
                    else:
                        last = nc.vector.scalar_tensor_tensor(out=new, in0=bank[rows, 0:T], scalar=bias[rows], in1=old,
                                                              op0=ALU.add, op1=ALU.add)
                last.then_inc(sems["state_ready"], 1)

            def dense(i, step):
                kind, s, ph, n = step
                bank = ps_dense[DENSE_NO[step] % DENSE_BANKS] if kind in DENSE else None
                what = PHASES[ph][1]
                if kind == "COPY":
                    dve.wait_ge(x_loaded[s], i * 16 + 16)
                    dve.wait_ge(stored[s], i * 16 + 16)
                    nc.vector.tensor_copy(x_sb[s][:], x_in[s][:]).then_inc(sems["x_taken"], 1)
                elif kind == "LNX":
                    before = last_step({"XADD", "COPY"}, step)
                    name = "x_taken" if before[0] == "COPY" else "x_ready"
                    dve.wait_ge(sems[name], count(i, name, before))
                    layer_norm(i, step, [x_sb[s][:, t] for t in range(TILES)])
                elif kind == "NORM":
                    before = last_step({"LNH", "LNX"}, step)
                    if before[0] == "LNH":
                        bank = ps_dense[DENSE_NO[before] % DENSE_BANKS]
                        normalise(i, step, [bank[:, P * t:P * (t + 1)] for t in range(TILES)])
                    else:
                        normalise(i, step, [x_sb[s][:, t] for t in range(TILES)])
                elif kind == "SPLIT":
                    if last_step({"STATE", "W2"}, step)[0] == "STATE":
                        dve.wait_ge(sems["state_set"], count(i, "state_set", last_step({"STATE"}, step)))
                    else:
                        dve.wait_ge(sems["state_ready"], count(i, "state_ready", last_step({"W2"}, step)))
                    nc.vector.tensor_copy(h_hi[s][:], state[s][:, 0:T]).then_inc(sems["vector_step"], 1)
                    dve.wait_ge(sems["vector_step"], count(i, "vector_step", step))
                    nc.vector.tensor_tensor(h_lo[s][:], state[s][:, 0:T], h_hi[s][:].bitcast(F32),
                                            ALU.subtract).then_inc(sems["split_ready"], 1)
                elif kind == "LNT":
                    dve.wait_ge(sems["high_ready"], count(i, "high_ready", step))
                    nc.vector.tensor_tensor(h_lo[s][:], bank[:, 0:T], h_hi[s][:].bitcast(F32),
                                            ALU.subtract).then_inc(sems["split_ready"], 1)
                elif kind == "Q":
                    u, t, m = ROPE_NO[step], n // 2, n % 2
                    table = rope[:, QKV_LAYER[what], t]
                    dve.wait_ge(sems["squares_ready"], count(i, "squares_ready", step))
                    if u >= ROPES:
                        dve.wait_ge(sems["rope_ready"], count(i, "rope_ready", ROPE_AT[u - ROPES]))
                    u %= ROPES
                    nc.vector.tensor_tensor(parts[:, u].rearrange("p o (h d) -> p o h d", d=LOCAL_D),
                                            bank[:].rearrange("p (o h d) -> p o h d", o=1, d=LOCAL_D).to_broadcast(
                                                [P, 2, LOCAL_HEADS, LOCAL_D]),
                                            table[:, :, m:m + 1].to_broadcast([P, 2, LOCAL_HEADS, LOCAL_D]),
                                            ALU.mult).then_inc(sems["rope_parts"], 1)
                    nc.vector.tensor_reduce(sums[:, u], squares[:, u].rearrange("p (h d) -> p h d", d=LOCAL_D), AX,
                                            ALU.add).then_inc(sems["vector_step"], 1)
                    dve.wait_ge(sems["vector_step"], count(i, "vector_step", step))
                    nc.vector.tensor_scalar(sums_floor[:, u], sums[:, u], NORM_FLOOR * NORM_FLOOR, None,
                                            ALU.max).then_inc(sems["squares_summed"], 1)
                elif kind == "QF":
                    dst, w = (stacked_q, stacked_k)[n // 2], n // 2
                    dve.wait_ge(sems["high_parts"], count(i, "high_parts", step))
                    for m in range(2):
                        c = 2 * (n % 2) + m
                        last = nc.vector.scalar_tensor_tensor(out=dst[s][:, c], in0=bank[:, T * m:T * (m + 1)],
                                                              scalar=biasf[:, w, c:c + 1], in1=high[:, m].bitcast(F32),
                                                              op0=ALU.add, op1=ALU.add)
                    last.then_inc(sems["stacked"], 1)
                elif kind == "W1":
                    l, rows = DENSE_LAYER[what], HID_ROWS[n]
                    dve.wait_ge(sems["gelu_ready"], count(i, "gelu_ready", step))
                    nc.vector.scalar_tensor_tensor(out=hidden[0:rows, n], in0=bank[0:rows, T:2 * T],
                                                   scalar=b1f[0:rows, l, n:n + 1], in1=gelu[0:rows, n],
                                                   op0=ALU.add, op1=ALU.mult).then_inc(sems["hidden_ready"], 1)
                else:
                    dve.wait_ge(sems["bank_filled"], count(i, "bank_filled", step))
                    if kind == "WO":
                        add_to_state(s, bank, None, None)
                    if kind == "LNH":
                        layer_norm(i, step, [bank[:, P * t:P * (t + 1)] for t in range(TILES)])
                    if kind == "W2":
                        l = DENSE_LAYER[what]
                        add_to_state(s, bank, y_t[s] if l == LAYERS - 1 else None, b2[:, l:l + 1])
                    if kind == "WOF":
                        nc.vector.tensor_scalar(y_t[s][:], bank[:, 0:T], bof[:, 0:1], None, ALU.add).then_inc(sems["state_ready"], 1)
                    if kind == "XADD":
                        nc.vector.scalar_tensor_tensor(out=x_sb[s][:].rearrange("p t c -> p (t c)"), in0=bank[:, 0:T],
                                                       scalar=1.0 if what == "from_full" else 0.5,
                                                       in1=x_sb[s][:].rearrange("p t c -> p (t c)"),
                                                       op0=ALU.mult, op1=ALU.add).then_inc(sems["x_ready"], 1)

            with dve.Fori(0, ITERS) as i:
                for step in DVE_ORDER:
                    if step[0] == "S":
                        row_max(i, step)
                    elif step[0] == "N":
                        scale_probs(i, step)
                    else:
                        dense(i, step)

        @block.tensor
        def _(pe):
            pe.wait_ge(w_loaded, 16 * N_WLOADS)
            for l in range(LAYERS):
                for m in range(2 * HC):
                    at, rows = w1_cols(m)
                    last = nc.tensor.matmul(ps_heads[0:rows, 2 * HC * l + m:2 * HC * l + m + 1], stage1[:, l, at:at + rows],
                                            lnb[:, l:l + 1], start=True, stop=True)
            last.then_inc(fold_summed, 1)
            pe.wait_ge(weights_ready, 1)
            pe.wait_ge(cleared, 1 + N_SELECTS)

            def split_matmul(dst, hi, lo, w_hi, w_lo, moving_weights):
                for n, (h, w) in enumerate(((hi, w_hi), (lo, w_hi), (hi, w_lo))):
                    lhs, rhs = (h, w) if moving_weights else (w, h)
                    last = nc.tensor.matmul(dst, lhs, rhs, start=(n == 0), stop=(n == 2))
                return last

            def scores(i, step):
                _, s, ph, h = step
                g = HEAD_NO[step]
                bank = ps_scores[g % SCORE_BANKS]
                if h == 0 and is_full(ph):
                    pe.wait_ge(sems["stacked"], count(i, "stacked", last_step({"QF"}, step)))
                elif h == 0:
                    pe.wait_ge(sems["qk_ready"], count(i, "qk_ready", last_step({"R"}, step)))
                if g >= SCORE_BANKS:
                    pe.wait_ge(sems["probs_ready"], count(i, "probs_ready", HEAD_AT[g - SCORE_BANKS]))
                if is_full(ph):
                    cols, mask, per, rows, key0 = FULL_COLS, mask_full, P // PAD_D, PAD_D, 0
                    at = PAD_D * (h % per)
                else:
                    cols, mask, per, rows, key0 = LOCAL_COLS, mask_local, 2, LOCAL_D, LOCAL_KEY0
                    at = LOCAL_D * (h % per)
                q, k = (stacked_q, stacked_k) if is_full(ph) else (q_t, k_t)
                q, k = q[s][at:at + rows, h // per], k[s][at:at + rows, h // per]
                for part, tok, keys in ((slice(0, P), slice(0, P), slice(0, P)), (slice(P, cols), slice(P, T), slice(key0, T))):
                    nc.tensor.matmul(bank[:, part], ident_b[:], mask[:, part], start=True, stop=False)
                    last = nc.tensor.matmul(bank[:, part], q[:, tok], k[:, keys], start=False, stop=True)
                last.then_inc(sems["scores_ready"], 1)

            def turn(i, step):
                g = head_no(step)
                bank, u = ps_turned[g % 2], g % PROBS
                if g >= 2:
                    pe.wait_ge(sems["turned_copied"], count(i, "turned_copied", ("T",) + HEAD_AT[g - 2][1:]))
                pe.wait_ge(sems["probs_scaled"], count(i, "probs_scaled", ("N",) + step[1:]))
                if is_full(step[2]):
                    for n in range(3):
                        last = nc.tensor.transpose(bank[:, P * n:P * (n + 1)], probs_full[:, u, P * n:P * (n + 1)], ident[:])
                else:
                    nc.tensor.transpose(bank[:, 0:P], probs_local[:, u, 0:P], ident[:])
                    nc.tensor.transpose(bank[:, P:P + WINDOW], probs_local[0:WINDOW, u, P:2 * P], ident[0:WINDOW, 0:WINDOW])
                    last = nc.tensor.transpose(bank[:, P + WINDOW:LOCAL_COLS], probs_local[:, u, 2 * P:3 * P], ident[:])
                last.then_inc(sems["probs_turned"], 1)

            def values(i, step):
                _, s, ph, n = step
                full = is_full(ph)
                pe.wait_ge(sems["turned_copied"], count(i, "turned_copied", ("T", s, ph, 2 * n + 1)))
                if n == 0:
                    pe.wait_ge(sems["values_ready"], count(i, "values_ready", last_step({"VAL", "VALF"}, step)))
                first = not full or n % 2 == 0
                if first and V_BEFORE[step] is not None:
                    pe.wait_ge(sems["heads_copied"], count(i, "heads_copied", V_BEFORE[step]))
                d = PAD_D if full else LOCAL_D
                k0 = T if full else P + WINDOW
                for t in range(TILES):
                    for h in (2 * n, 2 * n + 1):
                        at = d * (h % (P // d))
                        g = HEAD_NO[("S", s, ph, h)] % TURNED
                        cols, q0 = ((0, k0), 0) if t == 0 else ((k0, k0 + P), P)
                        last = nc.tensor.matmul(ps_heads[at:at + d, q0:q0 + cols[1] - cols[0]],
                                                val[s][:, t, d * h:d * (h + 1)], turned[:, g, cols[0]:cols[1]],
                                                start=(t == 0), stop=(t == TILES - 1), skip_group_check=True)
                last.then_inc(sems["heads_summed"], 1)

            def dense(i, step):
                kind, s, ph, n = step
                what = PHASES[ph][1]
                no = DENSE_NO[step]
                bank = ps_dense[no % DENSE_BANKS]
                if no >= DENSE_BANKS:
                    before = DENSE_AT[no - DENSE_BANKS]
                    if before[0] == "LNH":
                        before = ("NORM",) + before[1:]
                    pe.wait_ge(sems[RELEASES[before[0]]], count(i, RELEASES[before[0]], before))
                if kind in ("WO", "WOF"):
                    pe.wait_ge(sems["heads_copied"], count(i, "heads_copied", last_step({"V"}, step)))
                    w = wof if kind == "WOF" else wo[:, DENSE_LAYER[what]]
                    for c in range(CHUNKS):
                        last = nc.tensor.matmul(bank[:, 0:T], w[:, c], o_t[s][:, c], start=(c == 0), stop=(c == CHUNKS - 1))
                if kind == "LNH":
                    pe.wait_ge(sems["state_ready"], count(i, "state_ready", last_step({"WO"}, step)))
                    for t in range(TILES):
                        last = nc.tensor.transpose(bank[:, P * t:P * (t + 1)], state[s][:, P * t:P * (t + 1)], ident[:])
                if kind in ("LNT", "STATE"):
                    pe.wait_ge(sems["normed"], count(i, "normed", last_step({"NORM"}, step)))
                    for t in range(TILES):
                        last = nc.tensor.transpose(bank[:, P * t:P * (t + 1)], normal[s][:, t], ident[:])
                if kind == "XADD":
                    pe.wait_ge(sems["state_ready"], count(i, "state_ready", last_step({"W2", "WOF"}, step)))
                    for t in range(TILES):
                        last = nc.tensor.transpose(bank[:, P * t:P * (t + 1)], y_t[s][:, P * t:P * (t + 1)], ident[:])
                if kind in ("W1", "Q", "VAL", "QF", "VALF"):
                    pe.wait_ge(sems["split_ready"], count(i, "split_ready", last_step({"SPLIT", "LNT"}, step)))
                hi, lo = h_hi[s], h_lo[s]
                if kind == "W1":
                    l = DENSE_LAYER[what]
                    for m, at0 in ((HC + n, 0), (n, T)):
                        at, rows = w1_cols(m)
                        last = split_matmul(bank[0:rows, at0:at0 + T], hi[:], lo[:], w1_hi[:, l, at:at + rows],
                                            w1_lo[:, l, at:at + rows], False)
                if kind == "W2":
                    pe.wait_ge(sems["hidden_ready"], count(i, "hidden_ready", last_step({"W1"}, step)))
                    l = DENSE_LAYER[what]
                    for c, rows in enumerate(HID_ROWS):
                        last = nc.tensor.matmul(bank[:, 0:T], w2[0:rows, l, c], hidden[0:rows, c], start=(c == 0), stop=(c == HC - 1))
                if kind in ("Q", "VAL"):
                    l = QKV_LAYER[what]
                    t, m = (n // 2, n % 2) if kind == "Q" else (n, 2)
                    tok, cols = slice(P * t, P * (t + 1)), slice(INNER * m, INNER * (m + 1))
                    last = split_matmul(bank[:], hi[:, tok], lo[:, tok], wqkv_hi[:, l, cols], wqkv_lo[:, l, cols], True)
                if kind == "VALF":
                    tok = slice(P * n, P * (n + 1))
                    last = split_matmul(bank[:], hi[:, tok], lo[:, tok], wf_hi[:, 2], wf_lo[:, 2], True)
                if kind == "QF":
                    for m in range(2):
                        c = 2 * (n % 2) + m
                        cols = slice(P * c, P * (c + 1))
                        last = split_matmul(bank[:, T * m:T * (m + 1)], hi[:], lo[:], wf_hi[:, n // 2, cols],
                                            wf_lo[:, n // 2, cols], False)
                if kind == "R":
                    pe.wait_ge(sems["rope_ready"], count(i, "rope_ready", ("Q",) + step[1:]))
                    u = ROPE_NO[("Q",) + step[1:]] % ROPES
                    for c in range(CHUNKS):
                        last = nc.tensor.transpose(bank[:, P * c:P * (c + 1)], roped[:, u, P * c:P * (c + 1)], ident[:])
                last.then_inc(sems["bank_filled"], 1)

            with pe.Fori(0, ITERS) as i:
                for step in PE_ORDER:
                    if step[0] == "S":
                        scores(i, step)
                    elif step[0] == "T":
                        turn(i, step)
                    elif step[0] == "V":
                        values(i, step)
                    elif step[0] in DENSE:
                        dense(i, step)
                pe.wait_ge(sems["x_ready"], count(i, "x_ready", LAST))


_INS = ["L0_attn_x", "L0_attn_Wq", "L0_attn_bq", "L0_attn_Wk", "L0_attn_bk", "L0_attn_Wv", "L0_attn_bv", "L0_attn_Wo",
        "L0_attn_bo", "L0_ffn_wqkv", "L0_ffn_q_scale", "L0_ffn_k_scale", "L0_ffn_wo", "L0_ffn_ln_g", "L0_ffn_ln_b",
        "L0_ffn_w1", "L0_ffn_b1", "L0_ffn_w2", "L0_ffn_b2"]


def rope_table():
    half = np.arange(0, LOCAL_D, 2, dtype=np.float64)
    freqs = np.arange(T)[:, None] * (1.0 / 10000.0 ** (half / LOCAL_D))[None, :].astype(np.float32)
    freqs = np.concatenate([freqs, freqs], -1)
    base = (half + 0.4 * LOCAL_D) / (1.4 * LOCAL_D)
    power = (np.arange(T) - T // 2) / (WINDOW // 2)
    scale = base[None, :] ** power[:, None]
    scale = np.concatenate([scale, scale], -1)
    sign = np.where(np.arange(LOCAL_D) < LOCAL_D // 2, -1.0, 1.0)
    table = np.zeros((T, 2, 2, LOCAL_D))
    for m, s in enumerate((8.0 * scale, 1.0 / scale)):
        table[:, 0, m] = np.cos(freqs) * s
        table[:, 1, m] = np.roll(np.sin(freqs) * sign * s, LOCAL_D // 2, -1)
    return table.astype(np.float32)


def kernel(**inputs):
    import concourse.bacc as bacc
    from concourse.bass_utils import run_bass_kernel_spmd

    nc = bacc.Bacc("TRN2", target_bir_lowering=False, num_devices=1)
    arrays, args = {}, {}
    for name in _INS + ["rope"]:
        x = rope_table() if name == "rope" else np.ascontiguousarray(inputs[name])
        arrays[f"in_{name}_dram"] = x
        args[name] = nc.dram_tensor(f"in_{name}_dram", x.shape, mybir.dt.from_np(x.dtype), kind="ExternalInput").ap()
    out = nc.dram_tensor("out_0_dram", (SEQS, T, C), F32, kind="ExternalOutput").ap()
    macaron(nc, args, out)
    r = run_bass_kernel_spmd(nc, [arrays], core_ids=[0])
    return r.results[0]["out_0_dram"]
```

```python
from contextlib import ExitStack

import numpy as np

import concourse.bass as bass
from concourse import mybir

F32 = mybir.dt.float32
F32R = mybir.dt.float32r
BF16 = mybir.dt.bfloat16
ALU = mybir.AluOpType
ACT = mybir.ActivationFunctionType
AX = mybir.AxisListType.X
AXY = mybir.AxisListType.XY

P = 128
SEQS, T, C = 16, 256, 128
TILES = T // P
STREAMS = 4
LAYERS = 2
LOCAL_HEADS, LOCAL_D = 8, 64
WINDOW = 64
INNER = LOCAL_HEADS * LOCAL_D
HID = int(C * 4 * 2 / 3)
FULL_HEADS, FULL_D = 16, 8
PAD_D = 32
CHUNKS = INNER // P
HALF = C // 2
HID_ROWS = [min(P, HID - P * n) for n in range((HID + P - 1) // P)]
HC = len(HID_ROWS)
EPS = 1e-5
NORM_FLOOR = 1e-12
MASKED = -1e30
LOCAL_KEY0 = P - WINDOW
LOCAL_COLS = P + T - LOCAL_KEY0
FULL_COLS = P + T
STACKED = (0, 1, 2)
LOW_BLOCK = (1, 2)
FULL_SCALE = float(np.float32(1.0) / np.sqrt(np.float32(FULL_D)))
DENSE_BANKS = 3
SCORE_BANKS = 2
PROBS = 6
TURNED = 6
ROPES = 3

PHASES = [("D", "enter"), ("A", 0), ("D", "mid"), ("A", 1), ("D", "to_full"), ("A", "full"),
          ("D", "from_full"), ("A", 0), ("D", "mid"), ("A", 1), ("D", "leave"), ("D", "enter")]
LEAVE = 10
AHEAD = 11
AHEAD_STREAMS = 2
DENSE_LAYER = {"mid": 0, "to_full": 1, "leave": 1}
QKV_LAYER = {"enter": 0, "mid": 1, "from_full": 0}


def heads_of(phase):
    return FULL_HEADS if PHASES[phase][1] == "full" else LOCAL_HEADS


def is_full(phase):
    return PHASES[phase][1] == "full"


def dense_parts(s, ph):
    what = PHASES[ph][1]
    front, back = [], []
    if what == "enter":
        front += [("COPY", s, ph, 0)]
    if what in DENSE_LAYER:
        front += [("WO", s, ph, 0), ("LNH", s, ph, 0), ("NORM", s, ph, 0), ("LNT", s, ph, 0)]
        front += [("W1", s, ph, n) for n in range(HC)] + [("W2", s, ph, 0)]
    if what == "from_full":
        front += [("WOF", s, ph, 0)]
    if what in ("to_full", "from_full", "leave"):
        front += [("XADD", s, ph, 0)]
    if what in ("enter", "to_full", "from_full"):
        front += [("LNX", s, ph, 0), ("NORM", s, ph, 1)]
    if what in ("enter", "from_full"):
        front += [("STATE", s, ph, 0)]
    if what in QKV_LAYER:
        front += [("SPLIT", s, ph, 0)]
        back += [("Q", s, ph, 0), ("Q", s, ph, 1), ("VAL", s, ph, 0), ("Q", s, ph, 2), ("R", s, ph, 0),
                 ("Q", s, ph, 3), ("R", s, ph, 1), ("VAL", s, ph, 1), ("R", s, ph, 2), ("R", s, ph, 3)]
    if what == "to_full":
        front += [("LNT", s, ph, 1)]
        back += [("QF", s, ph, n) for n in range(4)] + [("VALF", s, ph, n) for n in range(TILES)]
    return front, back


def group_done(step):
    return not is_full(step[2]) or step[3] % 2 == 1


DENSE = {"WO", "LNH", "LNT", "W1", "W2", "WOF", "XADD", "STATE", "Q", "VAL", "R", "QF", "VALF"}
PE, ACTE, DVE, POOL = range(4)
PASSES = {
    "N": [(DVE, 0.64)], "T": [(PE, 0.35), (ACTE, 0.48)], "COPY": [(DVE, 0.2)], "SPLIT": [(DVE, 0.66)],
    "WO": [(PE, 1.9), (DVE, 0.67)], "LNH": [(PE, 0.22), (DVE, 0.9), (POOL, 0.2)], "LNX": [(DVE, 0.9), (POOL, 0.2)],
    "NORM": [(DVE, 0.66)], "LNT": [(PE, 0.22), (ACTE, 0.45), (DVE, 0.35)], "STATE": [(PE, 0.22), (ACTE, 0.85)],
    "W1": [(PE, 0.75), (ACTE, 0.45), (DVE, 0.4)], "W2": [(PE, 1.5), (DVE, 0.8)], "WOF": [(PE, 1.8), (DVE, 0.4)],
    "XADD": [(PE, 0.22), (DVE, 0.35)], "Q": [(PE, 0.7), (ACTE, 0.65), (DVE, 1.85), (POOL, 3.1)],
    "VAL": [(PE, 0.7), (ACTE, 0.65)], "VALF": [(PE, 0.7), (ACTE, 0.65)], "R": [(PE, 0.47), (ACTE, 0.65)],
    "QF": [(PE, 0.7), (ACTE, 1.1), (DVE, 0.75)]}
HANDOVER = 0.2
TABLE_CHANGE = 1.3
FRONT_AT, BACK_AT = -3.2, 14.9
PATIENCE = (0.0, 0.0, 0.0, 0.0)
PACE = (1.0, 1.0, 1.0, 1.0)
LATER_LOCAL = 0.0
FRONT_SHIFT = {0: 0.0, 2: -0.4, 4: 0.0, 6: 0.0, 8: 0.0, 10: 0.0, 11: -1.6}
BACK_SHIFT = {0: 0.0, 2: 0.0, 4: 0.0, 6: 0.0, 8: 0.0, 10: 0.0, 11: 0.0}
AHEAD_AT = 10.8
STORING = 3.0
SPACING = 0.35
LATER = {"S": 0.0, "N": 2.4, "T": 3.3, "V": 4.8}
URGENT = {"LNH": 4.0, "NORM": 4.0, "LNT": 5.6, "W1": 3.0, "W2": 5.7, "XADD": 1.2, "WO": 4.0, "WOF": 4.0,
           "SPLIT": -4.5, "STATE": 4.0,
          "LNX": 5.4, "N": -1.0, "T": -3.6, "V": -2.9, "VAL": 0.6, "VALF": -7.8, "R": -6.7, "QF": 0.8}


def passes(step):
    kind, _, ph, _ = step
    if kind == "S":
        return [(PE, 0.6), (DVE, 0.55), (ACTE, 0.75)] if is_full(ph) else [(PE, 0.75), (DVE, 0.47), (ACTE, 0.72)]
    if kind == "V":
        return [(PE, 0.5 if is_full(ph) else 0.65)] + ([(ACTE, 0.45)] if group_done(step) else [])
    return PASSES[kind]


def schedule(turns, dense):
    first = {}
    at = 0
    for turn in turns:
        first[turn] = at
        at += heads_of(turn[1])
    age, lines = {}, {"S": [], "N": [], "T": [], "V": [], "front": [], "back": []}
    for s, ph in turns:
        for h in range(heads_of(ph)):
            r = first[s, ph] + h
            for kind, n in (("S", h), ("N", h), ("T", h)) + ((("V", h // 2),) if h % 2 else ()):
                age[kind, s, ph, n] = r + LATER[kind] + (0.0 if is_full(ph) or kind == "S" else LATER_LOCAL)
                lines[kind].append((kind, s, ph, n))
    parts = []
    for s, ph in dense:
        if ph == 0:
            start = LOCAL_HEADS * (s - AHEAD_STREAMS) if turns else 0
        elif ph == AHEAD:
            start = first[s, LEAVE - 1] + LOCAL_HEADS + AHEAD_AT
        else:
            start = first[s, ph - 1] + heads_of(ph - 1)
        parts.append((start,) + dense_parts(s, ph))
    parts.sort(key=lambda x: (x[0], x[1][0][2] % AHEAD))
    after = {}

    def wait(step, part, other, other_part=-1, more=0.0):
        after.setdefault((step, part), []).append((other, other_part % len(passes(other)), more))

    for start, front, back in parts:
        lines["front"] += front
        lines["back"] += back
        for n, x in enumerate(front):
            age[x] = start + FRONT_AT + FRONT_SHIFT[x[2]] + SPACING * n
            if n and x[0] != "W1":
                wait(x, 0, front[n - 1])
            elif n:
                wait(x, 0, [y for y in front if y[0] == "LNT"][0])
        for n, x in enumerate(back):
            age[x] = start + BACK_AT + BACK_SHIFT[x[2]] + SPACING * n
            wait(x, 0, front[-1])
            if x[0] == "R":
                wait(x, 0, ("Q",) + x[1:])
        s, ph = front[0][1:3]
        if ph == AHEAD:
            wait(front[0], 0, ("XADD", s, LEAVE, 0), more=STORING)
        elif ph:
            wait(front[0], 0, ("V", s, ph - 1, heads_of(ph - 1) // 2 - 1))
        if ("S", s, ph + 1, 0) in age:
            for x in back:
                wait(("S", s, ph + 1, 0), 0, x)
        gates = [x for x in front if x[0] == "W1"]
        if gates:
            wait(gates[0], 1, gates[-1], 0)
            for x, y in zip(gates[1:], gates):
                wait(x, 1, y, 1)
    heads = lines["S"]
    for g, x in enumerate(heads):
        _, s, ph, h = x
        wait(("N",) + x[1:], 0, x)
        wait(("T",) + x[1:], 0, ("N",) + x[1:])
        if g >= SCORE_BANKS:
            wait(x, 0, heads[g - SCORE_BANKS])
        if g >= 2:
            wait(("T",) + x[1:], 0, ("T",) + heads[g - 2][1:])
        if g >= PROBS:
            wait(x, 2, ("T",) + heads[g - PROBS][1:], 0)
        if g >= TURNED:
            before = heads[g - TURNED]
            wait(("T",) + x[1:], 1, ("V",) + before[1:3] + (before[3] // 2,), 0)
    last_v = None
    for x in lines["V"]:
        wait(x, 0, ("T",) + x[1:3] + (2 * x[3] + 1,))
        if last_v is not None and (not is_full(x[2]) or x[3] % 2 == 0):
            wait(x, 0, last_v)
        if group_done(x):
            last_v = x
    ropes = [x for x in lines["back"] if x[0] == "Q"]
    for u, x in enumerate(ropes[ROPES:]):
        wait(x, 3, ("R",) + ropes[u][1:], 0)
        wait(x, 2, ropes[u])
        wait(x, 1, ropes[u], 2)

    waiting = [[] for _ in range(4)]
    for line in lines.values():
        for n, x in enumerate(line):
            for part, (engine, _) in enumerate(passes(x)):
                if part:
                    wait(x, part, x, part - 1)
                elif n:
                    wait(x, 0, line[n - 1], 0)
                waiting[engine].append((age[x] - (URGENT.get(x[0], 0.0) if engine != PE else 0.0), x, part))
    for w in waiting:
        w.sort(key=lambda y: y[0])
    done, free, orders, started = {}, [0.0] * 4, [[], [], [], []], {}
    filled, held, gelu_next = [], None, None
    while any(waiting):
        best = None
        for engine in range(4):
            choice = None
            for entry in waiting[engine][:60]:
                _, x, part = entry
                ready = 0.0
                if engine == PE and x[0] in DENSE:
                    if held is not None and x != held:
                        continue
                    if len(filled) >= DENSE_BANKS:
                        before = filled[-DENSE_BANKS]
                        if before[0] == "LNH":
                            before = ("NORM",) + before[1:]
                        release = (before, 2 if before[0] == "Q" else len(passes(before)) - 1)
                        if release not in done:
                            continue
                        ready = done[release] + HANDOVER
                if engine == ACTE and gelu_next is not None and x != gelu_next:
                    continue
                for b in after.get((x, part), ()):
                    if b[:2] not in done:
                        ready = None
                        break
                    ready = max(ready, done[b[:2]] + b[2] + (HANDOVER if passes(b[0])[b[1]][0] != engine else 0.0))
                if ready is None:
                    continue
                start = max(ready, free[engine])
                if choice is None or start < choice[0] - PATIENCE[engine]:
                    choice = (start, entry)
                if ready <= free[engine]:
                    break
            if choice is not None and (best is None or choice[0] < best[0]):
                best = (choice[0], engine, choice[1])
        start, engine, entry = best
        _, x, part = entry
        waiting[engine].remove(entry)
        lasts = passes(x)[part][1] * PACE[engine]
        if x[0] == "W1":
            more = x[:3] + (x[3] + 1,) if x[3] + 1 < HC else None
            if engine == PE:
                held = more
            if engine == ACTE:
                lasts += TABLE_CHANGE if x[3] in (0, HC - 1) else 0.0
                gelu_next = more
        if engine == PE and x[0] in DENSE:
            filled.append(x)
        done[x, part] = free[engine] = start + lasts
        if x not in started:
            started[x] = start
        orders[engine].append(x)
    order = sorted(started, key=lambda x: started[x])
    return [order] + orders


FIRST, PE_FIRST, ACT_FIRST, DVE_FIRST, POOL_FIRST = (
    sorted(order, key=lambda x: x[0] in ("Q", "VAL", "R"))
    for order in schedule([], [(s, 0) for s in range(AHEAD_STREAMS)]))
ORDER, PE_ORDER, ACT_ORDER, DVE_ORDER, POOL_ORDER = schedule(
    [(s, ph) for ph in range(1, LEAVE, 2) for s in range(STREAMS)],
    [(s, 0) for s in range(AHEAD_STREAMS, STREAMS)] + [(s, ph) for s in range(STREAMS) for ph in range(2, LEAVE + 1, 2)]
    + [(s, AHEAD) for s in range(AHEAD_STREAMS)])
assert len(set(FIRST + ORDER)) == len(FIRST + ORDER)


def last_step(kinds, step):
    steps = FIRST + ORDER
    for x in reversed(steps[:steps.index(step)]):
        if x[0] in kinds and x[1] == step[1]:
            return x
    raise ValueError(step)


def numbered(kinds):
    return {step: n for order in (PE_FIRST, PE_ORDER) for n, step in enumerate(x for x in order if x[0] in kinds)}


def earlier(numbers, buffers):
    out = {}
    for order in (PE_FIRST, PE_ORDER):
        at = {n: x for x, n in numbers.items() if x in set(order)}
        out.update({x: at[n - buffers] for n, x in at.items() if n >= buffers})
    return out


HEAD_NO = numbered({"S"})
DENSE_NO = numbered(DENSE)
ROPE_NO = numbered({"Q"})
HEAD_AT = {n: step for step, n in HEAD_NO.items()}
BANK_BEFORE = earlier(DENSE_NO, DENSE_BANKS)
ROPE_BEFORE = earlier(ROPE_NO, ROPES)


def emits(step):
    kind = step[0]
    out = {
        "S": {"scores_ready": 1, "max_ready": 1, "probs_ready": 1},
        "N": {"vector_step": 1, "probs_scaled": 1},
        "T": {"probs_turned": 1, "turned_copied": 1},
        "V": {"heads_summed": 1, "heads_copied": int(kind == "V" and group_done(step))},
        "COPY": {"x_taken": 1},
        "WO": {"state_ready": 1},
        "LNH": {"vector_step": 2, "var_ready": 1, "rstd_ready": 1},
        "LNX": {"vector_step": 2, "var_ready": 1, "rstd_ready": 1},
        "NORM": {"normed": 1},
        "LNT": {"high_ready": 1, "split_ready": 1},
        "W1": {"gelu_ready": 1, "hidden_ready": 1},
        "W2": {"state_ready": 1},
        "WOF": {"state_ready": 1},
        "XADD": {"x_ready": 1},
        "STATE": {"state_set": 1},
        "SPLIT": {"vector_step": 1, "split_ready": 1},
        "Q": {"squares_ready": 1, "squares_summed": 1, "rope_parts": 1, "vector_step": 1, "pool_step": 2, "rope_ready": 1},
        "VAL": {"values_ready": 1},
        "VALF": {"values_ready": 1},
        "R": {"qk_ready": 1},
        "QF": {"high_parts": 1, "stacked": 1},
    }[kind].copy()
    if kind in DENSE:
        out["bank_filled"] = 1
    return out


RELEASES = {"WO": "state_ready", "NORM": "normed", "LNT": "split_ready", "W1": "hidden_ready",
            "W2": "state_ready", "WOF": "state_ready", "XADD": "x_ready", "STATE": "state_set",
            "Q": "rope_parts", "VAL": "values_ready", "VALF": "values_ready", "R": "qk_ready",
            "QF": "stacked"}


COUNTED = (("scores_ready", "probs_turned", "heads_summed", "bank_filled"),
           ("probs_ready", "turned_copied", "heads_copied", "state_set", "high_ready", "squares_ready",
            "values_ready", "qk_ready", "gelu_ready", "high_parts"),
           ("max_ready", "vector_step", "probs_scaled", "x_taken", "state_ready", "var_ready", "normed",
            "split_ready", "hidden_ready", "x_ready", "squares_summed", "rope_parts", "stacked"),
           ("rstd_ready", "pool_step", "rope_ready"))
ALL_DONE = ("probs_ready", "turned_copied", "heads_copied", "state_set", "values_ready", "qk_ready", "state_ready",
            "normed", "split_ready", "hidden_ready", "x_ready", "rope_parts", "stacked")


def tally(orders):
    total, nth = {name: 0 for names in COUNTED for name in names}, {}
    for order, names in zip(orders, COUNTED):
        for step in order:
            for name, n in emits(step).items():
                if name in names and n:
                    total[name] += n
                    nth.setdefault(name, {})[step] = total[name]
    return total, nth


START, NTH_FIRST = tally((PE_FIRST, ACT_FIRST, DVE_FIRST, POOL_FIRST))
TOTAL, NTH = tally((PE_ORDER, ACT_ORDER, DVE_ORDER, POOL_ORDER))


V_BEFORE = {}
for _step in ORDER:
    if _step[0] == "V":
        V_BEFORE[_step] = next((x for x in reversed(ORDER[:ORDER.index(_step)]) if x[0] == "V" and group_done(x)), None)


def head_no(step):
    return HEAD_NO[("S",) + step[1:]]


def macaron(nc: bass.Bass, a, out):
    with ExitStack() as ctx:
        def sb(name, shape, dt=F32):
            return ctx.enter_context(nc.sbuf_tensor(name, shape, dt))

        def psum(name):
            return ctx.enter_context(nc.psum_tensor(name, [P, 512], F32))

        def sem(name):
            return ctx.enter_context(nc.semaphore(name))

        wqkv_hi = sb("wqkv_hi", [P, LAYERS, 3 * INNER], F32R)
        wqkv_lo = sb("wqkv_lo", [P, LAYERS, 3 * INNER], F32R)
        w1_hi = sb("w1_hi", [P, LAYERS, 2 * HID], F32R)
        w1_lo = sb("w1_lo", [P, LAYERS, 2 * HID], F32R)
        wf_hi = sb("wf_hi", [P, 3, FULL_HEADS * PAD_D], F32R)
        wf_lo = sb("wf_lo", [P, 3, FULL_HEADS * PAD_D], F32R)
        wo = sb("wo", [P, LAYERS, CHUNKS, C])
        w2 = sb("w2", [P, LAYERS, HC, C])
        wof = sb("wof", [P, CHUNKS, C])
        lng = sb("lng", [P, LAYERS])
        lnb = sb("lnb", [P, LAYERS])
        b1 = sb("b1", [P, LAYERS, 2 * HC])
        b1f = sb("b1f", [P, LAYERS, 2 * HC])
        b2 = sb("b2", [P, LAYERS])
        bof = sb("bof", [P, 1])
        biasf = sb("biasf", [P, 3, CHUNKS])
        low_rows = sb("low_rows", [P, 2])
        low_bias = sb("low_bias", [P, 2, CHUNKS])
        rope = sb("rope", [P, LAYERS, TILES, 2, 2, LOCAL_D])
        ident = sb("ident", [P, P])
        ident_b = sb("ident_b", [P, P], BF16)
        mask_local = sb("mask_local", [P, LOCAL_COLS], BF16)
        mask_full = sb("mask_full", [P, FULL_COLS], BF16)
        neg_half = sb("neg_half", [P, LOCAL_HEADS])
        neg_max = sb("neg_max", [P, PROBS, TILES])
        prob_sum = sb("prob_sum", [P, PROBS, TILES])
        prob_inv = sb("prob_inv", [P, PROBS, TILES])
        probs_local = sb("probs_local", [P, PROBS, P + T])

        def per_stream(name, shape, dt=F32, streams=range(STREAMS)):
            return [sb(f"{name}{s}", shape, dt) for s in streams]

        x_in = per_stream("x_in", [P, TILES, C])
        x_sb = per_stream("x_sb", [P, TILES, C])
        state = per_stream("state", [P, T + 1])
        y_t = per_stream("y_t", [P, T])

        normal = per_stream("normal", [P, TILES, C])
        bn = per_stream("bn", [P, TILES, 6])
        mean_var = per_stream("mean_var", [P, TILES, 2])
        var_eps = per_stream("var_eps", [P, TILES])
        rstd = per_stream("rstd", [P, TILES])
        h_hi = per_stream("h_hi", [P, T], F32R)
        h_lo = per_stream("h_lo", [P, T], F32R)

        squares = sb("squares", [P, ROPES, INNER])
        sums = sb("sums", [P, ROPES, LOCAL_HEADS])
        sums_floor = sb("sums_floor", [P, ROPES, LOCAL_HEADS])
        rnorm = sb("rnorm", [P, ROPES, LOCAL_HEADS])
        parts = sb("parts", [P, ROPES, 2, INNER])
        roped = sb("roped", [P, ROPES, INNER])

        def attention_buffers(streams):
            with ExitStack() as place:
                stacked = [place.enter_context(nc.sbuf_tensor(f"stacked_{m}{s}", [P, CHUNKS, T], F32R))
                           for m in "qk" for s in streams]
            plain = [sb(f"{m}_t{s}", [P, CHUNKS, T]) for m in "qk" for s in streams]
            n = len(streams)
            return stacked[:n], stacked[n:], plain[:n], plain[n:], per_stream("val", [P, TILES, INNER], F32, streams)

        first_streams = attention_buffers(range(AHEAD_STREAMS))

        with ExitStack() as setup:
            def staged(name, shape):
                return setup.enter_context(nc.sbuf_tensor(name, shape, F32))

            stage = staged("stage", [P, LAYERS, 3 * INNER])
            stage1 = staged("stage1", [P, LAYERS, 2 * HID])
            scaled1 = staged("scaled1", [P, LAYERS, 2 * HID])
            stagef = staged("stagef", [P, 3, C])
            padded = staged("padded", [P, 3, FULL_HEADS, PAD_D])
            rope_in = staged("rope_in", [P, TILES, 2, 2, LOCAL_D])
            qk_scale = staged("qk_scale", [P, 2, LAYERS, LOCAL_D])

        other_streams = attention_buffers(range(AHEAD_STREAMS, STREAMS))
        stacked_q, stacked_k, q_t, k_t, val = (a + b for a, b in zip(first_streams, other_streams))
        o_t = q_t
        gelu = sb("gelu", [P, HC, T])
        hidden = sb("hidden", [P, HC, T])
        high = sb("high", [P, 2, T], F32R)
        probs_full = sb("probs_full", [P, PROBS, P + T])
        turned = sb("turned", [P, TURNED, P + T])

        ps_scores = [psum(f"ps_scores{n}") for n in range(SCORE_BANKS)]
        ps_turned = [psum(f"ps_turned{n}") for n in range(2)]
        ps_heads = psum("ps_heads")
        ps_dense = [psum(f"ps_dense{n}") for n in range(DENSE_BANKS)]

        entry_loaded = sem("entry_loaded")
        w_loaded = sem("w_loaded")
        f_loaded = sem("f_loaded")
        x_loaded = [sem(f"x_loaded{s}") for s in range(STREAMS)]
        stored = [sem(f"stored{s}") for s in range(STREAMS)]
        cleared = sem("cleared")
        pads_cleared = sem("pads_cleared")
        fold_summed = sem("fold_summed")
        setup_step = sem("setup_step")
        entry_ready = sem("entry_ready")
        weights_ready = sem("weights_ready")
        sems = {name: sem(name) for name in TOTAL}

        def count(i, name, step, back=0):
            if i is None:
                return NTH_FIRST[name][step] - back
            if step in NTH_FIRST.get(name, {}):
                return i * TOTAL[name] + START[name]
            return i * TOTAL[name] + (START[name] + NTH[name][step] - back)

        block = ctx.enter_context(nc.Block())

        x_dram = a["L0_attn_x"].rearrange("(n s) (t p) c -> n s p t c", s=STREAMS, p=P)
        out_dram = out.rearrange("(n s) (t p) c -> n s p t c", s=STREAMS, p=P)
        ITERS = SEQS // STREAMS
        N_WLOADS = -1 + 2 * LAYERS + 3 + LAYERS * (3 + 2 * HC) + 4
        N_FLOADS = (2 * len(STACKED) + 2) * P // PAD_D
        N_CLEARED = 11

        def w1_cols(n):
            at = P * (n % HC) + (HID if n >= HC else 0)
            return at, HID_ROWS[n % HC]

        @block.sync
        def _(sp):
            def load_x(n, s):
                sp.dma_start(x_in[s][:], x_dram[n, s]).then_inc(x_loaded[s], 16)

            for s in range(AHEAD_STREAMS):
                load_x(0, s)
            n = 0

            def load(dst, src):
                sp.dma_start(dst, src).then_inc(w_loaded, 16)
                return 1

            with nc.allow_non_contiguous_dma(reason="bias columns, once"):
                sp.dma_start(rope_in[:], a["rope"].rearrange("(t p) a b d -> p t a b d", p=P)).then_inc(entry_loaded, 16)
                sp.dma_start(stage[:, 0], a["L0_ffn_wqkv"][0]).then_inc(entry_loaded, 16)
                for m, name in enumerate(("L0_ffn_q_scale", "L0_ffn_k_scale")):
                    for l in range(LAYERS):
                        src = a[name][l:l + 1].to_broadcast([P, LOCAL_D])
                        sp.dma_start(qk_scale[:, m, l], src).then_inc(stored[2 * m + l], 16)
                for s in range(AHEAD_STREAMS, STREAMS):
                    load_x(0, s)
                for l in range(LAYERS):
                    if l > 0:
                        n += load(stage[:, l], a["L0_ffn_wqkv"][l])
                    n += load(stage1[:, l], a["L0_ffn_w1"][l])
                for m, w in enumerate(("L0_attn_Wq", "L0_attn_Wk", "L0_attn_Wv")):
                    n += load(stagef[:, m], a[w])
                for l in range(LAYERS):
                    n += load(wo[:, l], a["L0_ffn_wo"][l].rearrange("(c p) n -> p c n", p=P))
                    full = HID // P
                    n += load(w2[:, l, 0:full], a["L0_ffn_w2"][l, 0:full * P].rearrange("(c p) n -> p c n", p=P))
                    n += load(w2[0:HID_ROWS[-1], l, full], a["L0_ffn_w2"][l, full * P:HID])
                    for m in range(2 * HC):
                        at, rows = w1_cols(m)
                        n += load(b1[0:rows, l, m:m + 1], a["L0_ffn_b1"][l, at:at + rows].rearrange("(p o) -> p o", o=1))
                for dst, src in ((lng, "L0_ffn_ln_g"), (lnb, "L0_ffn_ln_b"), (b2, "L0_ffn_b2")):
                    n += load(dst[:], a[src].rearrange("l p -> p l"))
                n += load(bof[:], a["L0_attn_bo"].rearrange("(p o) -> p o", o=1))
                assert n == N_WLOADS, n
                sp.wait_ge(pads_cleared, 1)
                m = 0
                for j in range(P // PAD_D):
                    rows = slice(PAD_D * j, PAD_D * j + FULL_D)
                    for b, name in enumerate(("L0_attn_bq", "L0_attn_bk", "L0_attn_bv")):
                        for part in STACKED if b < 2 else (0,):
                            at = PAD_D * j + FULL_D * part
                            sp.dma_start(biasf[at:at + FULL_D, b, :], a[name].rearrange("(c j d) -> j d c", j=4, d=FULL_D)[j]).then_inc(f_loaded, 16)
                            m += 1
                    sp.dma_start(wof[rows], a["L0_attn_Wo"].rearrange("(c j d) n -> j d c n", j=4, d=FULL_D)[j]).then_inc(f_loaded, 16)
                    m += 1
                assert m == N_FLOADS

            def store(i, s):
                sp.wait_ge(sems["x_ready"], count(i, "x_ready", ("XADD", s, LEAVE, 0)))
                sp.dma_start(out_dram[i, s], x_sb[s][:]).then_inc(stored[s], 16)

            def finish(i, ahead_next, late_next):
                if late_next is not None:
                    for s in range(AHEAD_STREAMS, STREAMS):
                        sp.wait_ge(sems["x_taken"], count(i, "x_taken", ("COPY", s, 0, 0)))
                        load_x(late_next, s)
                for s in range(STREAMS):
                    store(i, s)
                    if s < AHEAD_STREAMS and ahead_next is not None:
                        sp.wait_ge(sems["x_taken"], count(i, "x_taken", ("COPY", s, AHEAD, 0)))
                        load_x(ahead_next, s)

            for s in range(AHEAD_STREAMS):
                sp.wait_ge(sems["x_taken"], count(None, "x_taken", ("COPY", s, 0, 0)))
                load_x(1, s)
            with sp.Fori(0, ITERS - 2) as i:
                finish(i, i + 2, i + 1)
            finish(ITERS - 2, ITERS - 1, ITERS - 1)
            finish(ITERS - 1, None, None)
            for s in range(STREAMS):
                sp.wait_ge(stored[s], 16 * (ITERS + 1))

        @block.gpsimd
        def _(pool):
            nc.gpsimd.memset(neg_half[:], -0.5)
            nc.gpsimd.memset(ident[:], 0.0).then_inc(cleared, 1)
            pool.wait_ge(cleared, 1)
            n = 1

            def select(t, base, step, chan, op, fill):
                nonlocal n
                nc.gpsimd.affine_select(out=t, in_=t, compare_op=op, fill=fill, base=base,
                                        pattern=[[step, t.shape[1]]], channel_multiplier=chan).then_inc(cleared, 1)
                n += 1
                pool.wait_ge(cleared, n)

            select(ident[:], 0, -1, 1, ALU.not_equal, 1.0)
            nc.gpsimd.memset(padded[:], 0.0)
            nc.gpsimd.memset(biasf[:], 0.0)
            nc.gpsimd.memset(wof[:], 0.0).then_inc(pads_cleared, 1)

            def norm_scale(i, step):
                s = step[1]
                pool.wait_ge(sems["var_ready"], count(i, "var_ready", step))
                nc.gpsimd.tensor_tensor(rstd[s][:], var_eps[s][:], neg_half[:, 0:TILES], ALU.pow).then_inc(sems["rstd_ready"], 1)

            def rope_join(i, step):
                u = ROPE_NO[step] % ROPES
                pool.wait_ge(sems["rope_parts"], count(i, "rope_parts", step))
                joined = parts[:, u, 0].rearrange("p (h d) -> p h d", d=LOCAL_D)
                sines = parts[:, u, 1].rearrange("p (h d) -> p h d", d=LOCAL_D)
                hd = LOCAL_D // 2
                for half in range(2):
                    dst, src = slice(hd * half, hd * (half + 1)), slice(hd * (1 - half), hd * (2 - half))
                    last = nc.gpsimd.tensor_tensor(joined[:, :, dst], joined[:, :, dst], sines[:, :, src], ALU.add)
                last.then_inc(sems["pool_step"], 1)
                pool.wait_ge(sems["squares_summed"], count(i, "squares_summed", step))
                nc.gpsimd.tensor_tensor(rnorm[:, u], sums_floor[:, u], neg_half[:], ALU.pow).then_inc(sems["pool_step"], 1)
                if step in ROPE_BEFORE:
                    before = ROPE_BEFORE[step]
                    pool.wait_ge(sems["bank_filled"], count(i, "bank_filled", ("R",) + before[1:]))
                pool.wait_ge(sems["pool_step"], count(i, "pool_step", step))
                nc.gpsimd.tensor_tensor(roped[:, u].rearrange("p (h d) -> p h d", d=LOCAL_D),
                                        joined,
                                        rnorm[:, u].rearrange("p (h o) -> p h o", o=1).to_broadcast([P, LOCAL_HEADS, LOCAL_D]),
                                        ALU.mult).then_inc(sems["rope_ready"], 1)

            def take(i, step):
                if step[0] == "Q":
                    rope_join(i, step)
                else:
                    norm_scale(i, step)

            for step in POOL_FIRST:
                if step[0] != "Q":
                    take(None, step)
            nc.gpsimd.memset(ident_b[:], 0.0)
            nc.gpsimd.memset(mask_local[:], 0.0)
            nc.gpsimd.memset(mask_full[:], 0.0).then_inc(cleared, 1)
            n += 1
            pool.wait_ge(cleared, n)
            select(ident_b[:], 0, -1, 1, ALU.not_equal, 1.0)
            select(mask_local[:, 0:P], 0, -1, 1, ALU.is_ge, MASKED)
            select(mask_local[:, 0:P], WINDOW, 1, -1, ALU.is_ge, MASKED)
            select(mask_local[:, P:], 0, 1, -1, ALU.is_ge, MASKED)
            select(mask_local[:, P:], WINDOW, -1, 1, ALU.is_ge, MASKED)
            select(mask_full[:, 0:P], 0, -1, 1, ALU.is_ge, MASKED)
            select(mask_full[:, P:], P, -1, 1, ALU.is_ge, MASKED)
            nc.gpsimd.memset(probs_local[:], 0.0).then_inc(cleared, 1)
            n += 1
            assert n == N_CLEARED
            for step in POOL_FIRST:
                if step[0] == "Q":
                    take(None, step)
            with pool.Fori(0, ITERS) as i:
                for step in POOL_ORDER:
                    take(i, step)

        @block.scalar
        def _(act):
            def exp_scores(i, step):
                s, ph = step[1:3]
                g = HEAD_NO[step]
                u, bank = g % PROBS, ps_scores[g % SCORE_BANKS]
                act.wait_ge(sems["max_ready"], count(i, "max_ready", step))
                if g >= PROBS:
                    act.wait_ge(sems["probs_turned"], count(i, "probs_turned", ("T",) + HEAD_AT[g - PROBS][1:]))
                probs, at = (probs_full, P) if is_full(ph) else (probs_local, P + LOCAL_KEY0)
                cols = FULL_COLS if is_full(ph) else LOCAL_COLS
                for t, (dst, src) in enumerate(((probs[:, u, 0:P], bank[:, 0:P]),
                                                (probs[:, u, at:P + T], bank[:, P:cols]))):
                    last = nc.scalar.activation(dst, src, ACT.Exp, bias=neg_max[:, u, t:t + 1],
                                                accum_out=prob_sum[:, u, t:t + 1])
                last.then_inc(sems["probs_ready"], 1)

            def copy_turned(i, step):
                g = head_no(step)
                act.wait_ge(sems["probs_turned"], count(i, "probs_turned", step))
                if g >= TURNED:
                    h = HEAD_AT[g - TURNED]
                    act.wait_ge(sems["heads_summed"], count(i, "heads_summed", ("V", h[1], h[2], h[3] // 2)))
                cols = FULL_COLS if is_full(step[2]) else LOCAL_COLS
                nc.scalar.activation(turned[:, g % TURNED, 0:cols], ps_turned[g % 2][:, 0:cols],
                                     ACT.Copy).then_inc(sems["turned_copied"], 1)

            def copy_heads(i, step):
                s, ph, n = step[1:]
                act.wait_ge(sems["heads_summed"], count(i, "heads_summed", step))
                if is_full(ph):
                    c = n // 2
                    nc.scalar.activation(o_t[s][:, c], ps_heads[:, 0:T], ACT.Identity,
                                         bias=biasf[:, 2, c:c + 1]).then_inc(sems["heads_copied"], 1)
                else:
                    nc.scalar.activation(o_t[s][:, n], ps_heads[:, 0:T], ACT.Copy).then_inc(sems["heads_copied"], 1)

            def dense(i, step):
                kind, s, ph, n = step
                bank = ps_dense[DENSE_NO[step] % DENSE_BANKS]
                act.wait_ge(sems["bank_filled"], count(i, "bank_filled", step))
                if kind == "STATE":
                    nc.scalar.activation(state[s][0:HALF, 0:T], bank[0:HALF, 0:T], ACT.Copy)
                    nc.scalar.activation(state[s][HALF:C, 1:T + 1], bank[HALF:C, 0:T], ACT.Copy).then_inc(sems["state_set"], 1)
                if kind == "LNT":
                    nc.scalar.activation(h_hi[s][:], bank[:, 0:T], ACT.Copy).then_inc(sems["high_ready"], 1)
                if kind == "Q":
                    u = ROPE_NO[step]
                    if step in ROPE_BEFORE:
                        act.wait_ge(sems["squares_summed"], count(i, "squares_summed", ROPE_BEFORE[step]))
                    nc.scalar.activation(squares[:, u % ROPES], bank[:], ACT.Square).then_inc(sems["squares_ready"], 1)
                if kind in ("VAL", "VALF"):
                    nc.scalar.activation(val[s][:, n], bank[:], ACT.Copy).then_inc(sems["values_ready"], 1)
                if kind == "R":
                    dst = (q_t if n % 2 == 0 else k_t)[s]
                    nc.scalar.activation(dst[:, :, P * (n // 2):P * (n // 2 + 1)],
                                         bank[:].rearrange("p (c q) -> p c q", c=CHUNKS), ACT.Copy).then_inc(sems["qk_ready"], 1)
                if kind == "QF":
                    if n > 0:
                        act.wait_ge(sems["stacked"], count(i, "stacked", ("QF", s, ph, n - 1)))
                    w = n // 2
                    for m in range(2):
                        c = 2 * (n % 2) + m
                        last = nc.scalar.activation(high[:, m], bank[:, T * m:T * (m + 1)], ACT.Identity,
                                                    bias=low_bias[:, w, c:c + 1], scale=low_rows[:, w:w + 1])
                    last.then_inc(sems["high_parts"], 1)
                if kind == "W1":
                    l, rows = DENSE_LAYER[PHASES[ph][1]], HID_ROWS[n]
                    nc.scalar.activation(gelu[0:rows, n], bank[0:rows, 0:T], ACT.Gelu,
                                         bias=b1f[0:rows, l, HC + n:HC + n + 1]).then_inc(sems["gelu_ready"], 1)

            for step in ACT_FIRST:
                dense(None, step)
            act.wait_ge(weights_ready, 1)
            with act.Fori(0, ITERS) as i:
                for step in ACT_ORDER:
                    if step[0] == "S":
                        exp_scores(i, step)
                    elif step[0] == "T":
                        copy_turned(i, step)
                    elif step[0] == "V":
                        copy_heads(i, step)
                    else:
                        dense(i, step)

        @block.vector
        def _(dve):
            links = [0]

            def link(ins):
                links[0] += 1
                ins.then_inc(setup_step, 1)
                dve.wait_ge(setup_step, links[0])

            def turn_table(l):
                for t in range(TILES):
                    last = nc.vector.tensor_tensor(rope[:, l, t], rope_in[:, t],
                                                   qk_scale[:, :, l].rearrange("p (o m) d -> p o m d", o=1).to_broadcast(
                                                       [P, 2, 2, LOCAL_D]), ALU.mult)
                return last

            def prepare_entry():
                dve.wait_ge(entry_loaded, 32)
                for s in range(STREAMS):
                    dve.wait_ge(stored[s], 16)
                link(nc.vector.tensor_copy(wqkv_hi[:, 0], stage[:, 0]))
                turn_table(0)
                nc.vector.tensor_tensor(wqkv_lo[:, 0], stage[:, 0], wqkv_hi[:, 0].bitcast(F32),
                                        ALU.subtract).then_inc(entry_ready, 1)
                dve.wait_ge(entry_ready, 1)

            def prepare(part):
                if part == 0:
                    dve.wait_ge(w_loaded, 16 * N_WLOADS)
                    dve.wait_ge(pads_cleared, 1)
                    nc.vector.tensor_copy(wqkv_hi[:, 1:], stage[:, 1:])
                    for l in range(LAYERS):
                        last = nc.vector.tensor_scalar(scaled1[:, l], stage1[:, l], lng[:, l:l + 1], None, ALU.mult)
                    link(last)
                if part == 1:
                    nc.vector.tensor_copy(w1_hi[:], scaled1[:])
                    for m in range(3):
                        for block in STACKED if m < 2 else (0,):
                            last = nc.vector.tensor_scalar(padded[:, m, :, FULL_D * block:FULL_D * (block + 1)],
                                                           stagef[:, m].rearrange("p (h d) -> p h d", d=FULL_D),
                                                           FULL_SCALE if m == 0 else 1.0, None, ALU.mult)
                    link(last)
                if part == 2:
                    link(nc.vector.tensor_copy(wf_hi[:], padded[:].rearrange("p m h d -> p m (h d)")))
                    nc.vector.tensor_tensor(wqkv_lo[:, 1:], stage[:, 1:], wqkv_hi[:, 1:].bitcast(F32), ALU.subtract)
                if part == 3:
                    for l in range(1, LAYERS):
                        turn_table(l)
                    nc.vector.tensor_tensor(w1_lo[:], scaled1[:], w1_hi[:].bitcast(F32), ALU.subtract)
                    link(nc.vector.tensor_tensor(wf_lo[:], padded[:].rearrange("p m h d -> p m (h d)"),
                                                 wf_hi[:].bitcast(F32), ALU.subtract))

            def prepare_biases():
                dve.wait_ge(fold_summed, 1)
                for l in range(LAYERS):
                    for m in range(2 * HC):
                        rows = w1_cols(m)[1]
                        nc.vector.tensor_tensor(b1f[0:rows, l, m:m + 1], b1[0:rows, l, m:m + 1],
                                                ps_heads[0:rows, 2 * HC * l + m:2 * HC * l + m + 1], ALU.add)
                dve.wait_ge(f_loaded, 16 * N_FLOADS)
                nc.vector.tensor_scalar(biasf[:, 0], biasf[:, 0], FULL_SCALE, None, ALU.mult)
                for m, block in enumerate(LOW_BLOCK):
                    ones = ident[:].rearrange("p (j r) -> p j r", r=PAD_D)[:, :, FULL_D * block:FULL_D * (block + 1)]
                    last = nc.vector.tensor_reduce(low_rows[:, m:m + 1], ones, AXY, ALU.add, negate=True)
                link(last)
                for m in range(2):
                    last = nc.vector.tensor_scalar(low_bias[:, m], biasf[:, m], low_rows[:, m:m + 1], None, ALU.mult)
                last.then_inc(weights_ready, 1)
                dve.wait_ge(weights_ready, 1)
                dve.wait_ge(cleared, N_CLEARED)

            def row_max(i, step):
                g = HEAD_NO[step]
                u, bank = g % PROBS, ps_scores[g % SCORE_BANKS]
                cols = FULL_COLS if is_full(step[2]) else LOCAL_COLS
                dve.wait_ge(sems["scores_ready"], count(i, "scores_ready", step))
                nc.vector.tensor_reduce(neg_max[:, u, 0:1], bank[:, 0:P], AX, ALU.max, negate=True)
                nc.vector.tensor_reduce(neg_max[:, u, 1:2], bank[:, P:cols], AX, ALU.max,
                                        negate=True).then_inc(sems["max_ready"], 1)

            def scale_probs(i, step):
                u = head_no(step) % PROBS
                probs, at = (probs_full, P) if is_full(step[2]) else (probs_local, P + LOCAL_KEY0)
                dve.wait_ge(sems["probs_ready"], count(i, "probs_ready", ("S",) + step[1:]))
                nc.vector.reciprocal(prob_inv[:, u], prob_sum[:, u]).then_inc(sems["vector_step"], 1)
                dve.wait_ge(sems["vector_step"], count(i, "vector_step", step))
                nc.vector.tensor_scalar(probs[:, u, 0:P], probs[:, u, 0:P], prob_inv[:, u, 0:1], None, ALU.mult)
                nc.vector.tensor_scalar(probs[:, u, at:P + T], probs[:, u, at:P + T], prob_inv[:, u, 1:2], None,
                                        ALU.mult).then_inc(sems["probs_scaled"], 1)

            def layer_norm(i, step, source):
                s = step[1]
                for t in range(TILES):
                    last = nc.vector.bn_stats(bn[s][:, t], source[t])
                last.then_inc(sems["vector_step"], 1)
                dve.wait_ge(sems["vector_step"], count(i, "vector_step", step, 1))
                nc.vector.memset(var_eps[s][:], 0.0)
                for t in range(TILES):
                    last = nc.vector.bn_aggr(mean_var[s][:, t], bn[s][:, t])
                last.then_inc(sems["vector_step"], 1)
                dve.wait_ge(sems["vector_step"], count(i, "vector_step", step))
                nc.vector.tensor_scalar(var_eps[s][:], mean_var[s][:, :, 1], EPS, None, ALU.add).then_inc(sems["var_ready"], 1)

            def normalise(i, step, source):
                s = step[1]
                dve.wait_ge(sems["rstd_ready"], count(i, "rstd_ready", last_step({"LNH", "LNX"}, step)))
                for t in range(TILES):
                    last = nc.vector.tensor_scalar(normal[s][:, t], source[t], mean_var[s][:, t, 0:1], rstd[s][:, t:t + 1],
                                                   ALU.subtract, ALU.mult)
                last.then_inc(sems["normed"], 1)

            def add_to_state(s, bank, dst, bias):
                for rows, at in ((slice(0, HALF), 0), (slice(HALF, C), 1)):
                    old = state[s][rows, at:at + T]
                    new = dst[rows, :] if dst is not None else old
                    if bias is None:
                        last = nc.vector.tensor_tensor(new, bank[rows, 0:T], old, ALU.add)
                    else:
                        last = nc.vector.scalar_tensor_tensor(out=new, in0=bank[rows, 0:T], scalar=bias[rows], in1=old,
                                                              op0=ALU.add, op1=ALU.add)
                last.then_inc(sems["state_ready"], 1)

            def dense(i, step):
                kind, s, ph, n = step
                bank = ps_dense[DENSE_NO[step] % DENSE_BANKS] if kind in DENSE else None
                what = PHASES[ph][1]
                if kind == "COPY":
                    if i is None:
                        dve.wait_ge(x_loaded[s], 16)
                    else:
                        dve.wait_ge(x_loaded[s], i * 16 + (32 if ph == AHEAD else 16))
                        dve.wait_ge(stored[s], i * 16 + (32 if ph == AHEAD else 16))
                    nc.vector.tensor_copy(x_sb[s][:], x_in[s][:]).then_inc(sems["x_taken"], 1)
                elif kind == "LNX":
                    before = last_step({"XADD", "COPY"}, step)
                    name = "x_taken" if before[0] == "COPY" else "x_ready"
                    dve.wait_ge(sems[name], count(i, name, before))
                    layer_norm(i, step, [x_sb[s][:, t] for t in range(TILES)])
                elif kind == "NORM":
                    before = last_step({"LNH", "LNX"}, step)
                    if before[0] == "LNH":
                        bank = ps_dense[DENSE_NO[before] % DENSE_BANKS]
                        normalise(i, step, [bank[:, P * t:P * (t + 1)] for t in range(TILES)])
                    else:
                        normalise(i, step, [x_sb[s][:, t] for t in range(TILES)])
                elif kind == "SPLIT":
                    if last_step({"STATE", "W2"}, step)[0] == "STATE":
                        dve.wait_ge(sems["state_set"], count(i, "state_set", last_step({"STATE"}, step)))
                    else:
                        dve.wait_ge(sems["state_ready"], count(i, "state_ready", last_step({"W2"}, step)))
                    nc.vector.tensor_copy(h_hi[s][:], state[s][:, 0:T]).then_inc(sems["vector_step"], 1)
                    dve.wait_ge(sems["vector_step"], count(i, "vector_step", step))
                    nc.vector.tensor_tensor(h_lo[s][:], state[s][:, 0:T], h_hi[s][:].bitcast(F32),
                                            ALU.subtract).then_inc(sems["split_ready"], 1)
                elif kind == "LNT":
                    dve.wait_ge(sems["high_ready"], count(i, "high_ready", step))
                    nc.vector.tensor_tensor(h_lo[s][:], bank[:, 0:T], h_hi[s][:].bitcast(F32),
                                            ALU.subtract).then_inc(sems["split_ready"], 1)
                elif kind == "Q":
                    u, t, m = ROPE_NO[step], n // 2, n % 2
                    table = rope[:, QKV_LAYER[what], t]
                    dve.wait_ge(sems["squares_ready"], count(i, "squares_ready", step))
                    if step in ROPE_BEFORE:
                        dve.wait_ge(sems["rope_ready"], count(i, "rope_ready", ROPE_BEFORE[step]))
                    u %= ROPES
                    nc.vector.tensor_tensor(parts[:, u].rearrange("p o (h d) -> p o h d", d=LOCAL_D),
                                            bank[:].rearrange("p (o h d) -> p o h d", o=1, d=LOCAL_D).to_broadcast(
                                                [P, 2, LOCAL_HEADS, LOCAL_D]),
                                            table[:, :, m:m + 1].to_broadcast([P, 2, LOCAL_HEADS, LOCAL_D]),
                                            ALU.mult).then_inc(sems["rope_parts"], 1)
                    nc.vector.tensor_reduce(sums[:, u], squares[:, u].rearrange("p (h d) -> p h d", d=LOCAL_D), AX,
                                            ALU.add).then_inc(sems["vector_step"], 1)
                    dve.wait_ge(sems["vector_step"], count(i, "vector_step", step))
                    nc.vector.tensor_scalar(sums_floor[:, u], sums[:, u], NORM_FLOOR * NORM_FLOOR, None,
                                            ALU.max).then_inc(sems["squares_summed"], 1)
                elif kind == "QF":
                    dst, w = (stacked_q, stacked_k)[n // 2], n // 2
                    dve.wait_ge(sems["high_parts"], count(i, "high_parts", step))
                    for m in range(2):
                        c = 2 * (n % 2) + m
                        last = nc.vector.scalar_tensor_tensor(out=dst[s][:, c], in0=bank[:, T * m:T * (m + 1)],
                                                              scalar=biasf[:, w, c:c + 1], in1=high[:, m].bitcast(F32),
                                                              op0=ALU.add, op1=ALU.add)
                    last.then_inc(sems["stacked"], 1)
                elif kind == "W1":
                    l, rows = DENSE_LAYER[what], HID_ROWS[n]
                    dve.wait_ge(sems["gelu_ready"], count(i, "gelu_ready", step))
                    nc.vector.scalar_tensor_tensor(out=hidden[0:rows, n], in0=bank[0:rows, T:2 * T],
                                                   scalar=b1f[0:rows, l, n:n + 1], in1=gelu[0:rows, n],
                                                   op0=ALU.add, op1=ALU.mult).then_inc(sems["hidden_ready"], 1)
                else:
                    dve.wait_ge(sems["bank_filled"], count(i, "bank_filled", step))
                    if kind == "WO":
                        add_to_state(s, bank, None, None)
                    if kind == "LNH":
                        layer_norm(i, step, [bank[:, P * t:P * (t + 1)] for t in range(TILES)])
                    if kind == "W2":
                        l = DENSE_LAYER[what]
                        add_to_state(s, bank, y_t[s] if l == LAYERS - 1 else None, b2[:, l:l + 1])
                    if kind == "WOF":
                        nc.vector.tensor_scalar(y_t[s][:], bank[:, 0:T], bof[:, 0:1], None, ALU.add).then_inc(sems["state_ready"], 1)
                    if kind == "XADD":
                        nc.vector.scalar_tensor_tensor(out=x_sb[s][:].rearrange("p t c -> p (t c)"), in0=bank[:, 0:T],
                                                       scalar=1.0 if what == "from_full" else 0.5,
                                                       in1=x_sb[s][:].rearrange("p t c -> p (t c)"),
                                                       op0=ALU.mult, op1=ALU.add).then_inc(sems["x_ready"], 1)

            for s in range(STREAMS):
                nc.vector.memset(state[s][HALF:C, 0:1], 0.0)
            projections = 0
            for step in DVE_FIRST:
                if step[0] == "Q":
                    if projections == 0:
                        prepare_entry()
                    dense(None, step)
                    if projections > 0:
                        prepare(projections - 1)
                    projections += 1
                else:
                    dense(None, step)
            prepare_biases()
            with dve.Fori(0, ITERS) as i:
                for step in DVE_ORDER:
                    if step[0] == "S":
                        row_max(i, step)
                    elif step[0] == "N":
                        scale_probs(i, step)
                    else:
                        dense(i, step)

        @block.tensor
        def _(pe):
            def split_matmul(dst, hi, lo, w_hi, w_lo, moving_weights):
                for n, (h, w) in enumerate(((hi, w_hi), (lo, w_hi), (hi, w_lo))):
                    lhs, rhs = (h, w) if moving_weights else (w, h)
                    last = nc.tensor.matmul(dst, lhs, rhs, start=(n == 0), stop=(n == 2))
                return last

            def scores(i, step):
                _, s, ph, h = step
                g = HEAD_NO[step]
                bank = ps_scores[g % SCORE_BANKS]
                if h == 0 and is_full(ph):
                    pe.wait_ge(sems["stacked"], count(i, "stacked", last_step({"QF"}, step)))
                elif h == 0:
                    pe.wait_ge(sems["qk_ready"], count(i, "qk_ready", last_step({"R"}, step)))
                if g >= SCORE_BANKS:
                    pe.wait_ge(sems["probs_ready"], count(i, "probs_ready", HEAD_AT[g - SCORE_BANKS]))
                if is_full(ph):
                    cols, mask, per, rows, key0 = FULL_COLS, mask_full, P // PAD_D, PAD_D, 0
                    at = PAD_D * (h % per)
                else:
                    cols, mask, per, rows, key0 = LOCAL_COLS, mask_local, 2, LOCAL_D, LOCAL_KEY0
                    at = LOCAL_D * (h % per)
                q, k = (stacked_q, stacked_k) if is_full(ph) else (q_t, k_t)
                q, k = q[s][at:at + rows, h // per], k[s][at:at + rows, h // per]
                for part, tok, keys in ((slice(0, P), slice(0, P), slice(0, P)), (slice(P, cols), slice(P, T), slice(key0, T))):
                    nc.tensor.matmul(bank[:, part], ident_b[:], mask[:, part], start=True, stop=False)
                    last = nc.tensor.matmul(bank[:, part], q[:, tok], k[:, keys], start=False, stop=True)
                last.then_inc(sems["scores_ready"], 1)

            def turn(i, step):
                g = head_no(step)
                bank, u = ps_turned[g % 2], g % PROBS
                if g >= 2:
                    pe.wait_ge(sems["turned_copied"], count(i, "turned_copied", ("T",) + HEAD_AT[g - 2][1:]))
                pe.wait_ge(sems["probs_scaled"], count(i, "probs_scaled", ("N",) + step[1:]))
                if is_full(step[2]):
                    for n in range(3):
                        last = nc.tensor.transpose(bank[:, P * n:P * (n + 1)], probs_full[:, u, P * n:P * (n + 1)], ident[:])
                else:
                    nc.tensor.transpose(bank[:, 0:P], probs_local[:, u, 0:P], ident[:])
                    nc.tensor.transpose(bank[:, P:P + WINDOW], probs_local[0:WINDOW, u, P:2 * P], ident[0:WINDOW, 0:WINDOW])
                    last = nc.tensor.transpose(bank[:, P + WINDOW:LOCAL_COLS], probs_local[:, u, 2 * P:3 * P], ident[:])
                last.then_inc(sems["probs_turned"], 1)

            def values(i, step):
                _, s, ph, n = step
                full = is_full(ph)
                pe.wait_ge(sems["turned_copied"], count(i, "turned_copied", ("T", s, ph, 2 * n + 1)))
                if n == 0:
                    pe.wait_ge(sems["values_ready"], count(i, "values_ready", last_step({"VAL", "VALF"}, step)))
                first = not full or n % 2 == 0
                if first and V_BEFORE[step] is not None:
                    pe.wait_ge(sems["heads_copied"], count(i, "heads_copied", V_BEFORE[step]))
                d = PAD_D if full else LOCAL_D
                k0 = T if full else P + WINDOW
                for t in range(TILES):
                    for h in (2 * n, 2 * n + 1):
                        at = d * (h % (P // d))
                        g = HEAD_NO[("S", s, ph, h)] % TURNED
                        cols, q0 = ((0, k0), 0) if t == 0 else ((k0, k0 + P), P)
                        last = nc.tensor.matmul(ps_heads[at:at + d, q0:q0 + cols[1] - cols[0]],
                                                val[s][:, t, d * h:d * (h + 1)], turned[:, g, cols[0]:cols[1]],
                                                start=(t == 0), stop=(t == TILES - 1), skip_group_check=True)
                last.then_inc(sems["heads_summed"], 1)

            def dense(i, step):
                kind, s, ph, n = step
                what = PHASES[ph][1]
                bank = ps_dense[DENSE_NO[step] % DENSE_BANKS]
                if step in BANK_BEFORE:
                    before = BANK_BEFORE[step]
                    if before[0] == "LNH":
                        before = ("NORM",) + before[1:]
                    pe.wait_ge(sems[RELEASES[before[0]]], count(i, RELEASES[before[0]], before))
                if kind in ("WO", "WOF"):
                    pe.wait_ge(sems["heads_copied"], count(i, "heads_copied", last_step({"V"}, step)))
                    w = wof if kind == "WOF" else wo[:, DENSE_LAYER[what]]
                    for c in range(CHUNKS):
                        last = nc.tensor.matmul(bank[:, 0:T], w[:, c], o_t[s][:, c], start=(c == 0), stop=(c == CHUNKS - 1))
                if kind == "LNH":
                    pe.wait_ge(sems["state_ready"], count(i, "state_ready", last_step({"WO"}, step)))
                    for t in range(TILES):
                        last = nc.tensor.transpose(bank[:, P * t:P * (t + 1)], state[s][:, P * t:P * (t + 1)], ident[:])
                if kind in ("LNT", "STATE"):
                    pe.wait_ge(sems["normed"], count(i, "normed", last_step({"NORM"}, step)))
                    for t in range(TILES):
                        last = nc.tensor.transpose(bank[:, P * t:P * (t + 1)], normal[s][:, t], ident[:])
                if kind == "XADD":
                    pe.wait_ge(sems["state_ready"], count(i, "state_ready", last_step({"W2", "WOF"}, step)))
                    for t in range(TILES):
                        last = nc.tensor.transpose(bank[:, P * t:P * (t + 1)], y_t[s][:, P * t:P * (t + 1)], ident[:])
                if kind in ("W1", "Q", "VAL", "QF", "VALF"):
                    pe.wait_ge(sems["split_ready"], count(i, "split_ready", last_step({"SPLIT", "LNT"}, step)))
                hi, lo = h_hi[s], h_lo[s]
                if kind == "W1":
                    l = DENSE_LAYER[what]
                    for m, at0 in ((HC + n, 0), (n, T)):
                        at, rows = w1_cols(m)
                        last = split_matmul(bank[0:rows, at0:at0 + T], hi[:], lo[:], w1_hi[:, l, at:at + rows],
                                            w1_lo[:, l, at:at + rows], False)
                if kind == "W2":
                    pe.wait_ge(sems["hidden_ready"], count(i, "hidden_ready", last_step({"W1"}, step)))
                    l = DENSE_LAYER[what]
                    for c, rows in enumerate(HID_ROWS):
                        last = nc.tensor.matmul(bank[:, 0:T], w2[0:rows, l, c], hidden[0:rows, c], start=(c == 0), stop=(c == HC - 1))
                if kind in ("Q", "VAL"):
                    l = QKV_LAYER[what]
                    t, m = (n // 2, n % 2) if kind == "Q" else (n, 2)
                    tok, cols = slice(P * t, P * (t + 1)), slice(INNER * m, INNER * (m + 1))
                    last = split_matmul(bank[:], hi[:, tok], lo[:, tok], wqkv_hi[:, l, cols], wqkv_lo[:, l, cols], True)
                if kind == "VALF":
                    tok = slice(P * n, P * (n + 1))
                    last = split_matmul(bank[:], hi[:, tok], lo[:, tok], wf_hi[:, 2], wf_lo[:, 2], True)
                if kind == "QF":
                    for m in range(2):
                        c = 2 * (n % 2) + m
                        cols = slice(P * c, P * (c + 1))
                        last = split_matmul(bank[:, T * m:T * (m + 1)], hi[:], lo[:], wf_hi[:, n // 2, cols],
                                            wf_lo[:, n // 2, cols], False)
                if kind == "R":
                    pe.wait_ge(sems["rope_ready"], count(i, "rope_ready", ("Q",) + step[1:]))
                    u = ROPE_NO[("Q",) + step[1:]] % ROPES
                    for c in range(CHUNKS):
                        last = nc.tensor.transpose(bank[:, P * c:P * (c + 1)], roped[:, u, P * c:P * (c + 1)], ident[:])
                last.then_inc(sems["bank_filled"], 1)

            def wait_for_all(i):
                for name in ALL_DONE:
                    if i is None and START[name]:
                        pe.wait_ge(sems[name], START[name])
                    elif i is not None:
                        pe.wait_ge(sems[name], i * TOTAL[name] + (START[name] + TOTAL[name]))

            pe.wait_ge(cleared, 2)
            for step in PE_FIRST:
                if step[0] == "Q":
                    pe.wait_ge(entry_ready, 1)
                dense(None, step)
            pe.wait_ge(w_loaded, 16 * N_WLOADS)
            for l in range(LAYERS):
                for m in range(2 * HC):
                    at, rows = w1_cols(m)
                    last = nc.tensor.matmul(ps_heads[0:rows, 2 * HC * l + m:2 * HC * l + m + 1], stage1[:, l, at:at + rows],
                                            lnb[:, l:l + 1], start=True, stop=True)
            last.then_inc(fold_summed, 1)
            pe.wait_ge(weights_ready, 1)
            pe.wait_ge(cleared, N_CLEARED)
            wait_for_all(None)
            with pe.Fori(0, ITERS) as i:
                for step in PE_ORDER:
                    if step[0] == "S":
                        scores(i, step)
                    elif step[0] == "T":
                        turn(i, step)
                    elif step[0] == "V":
                        values(i, step)
                    else:
                        dense(i, step)
                wait_for_all(i)


_INS = ["L0_attn_x", "L0_attn_Wq", "L0_attn_bq", "L0_attn_Wk", "L0_attn_bk", "L0_attn_Wv", "L0_attn_bv", "L0_attn_Wo",
        "L0_attn_bo", "L0_ffn_wqkv", "L0_ffn_q_scale", "L0_ffn_k_scale", "L0_ffn_wo", "L0_ffn_ln_g", "L0_ffn_ln_b",
        "L0_ffn_w1", "L0_ffn_b1", "L0_ffn_w2", "L0_ffn_b2"]


def rope_table():
    half = np.arange(0, LOCAL_D, 2, dtype=np.float64)
    freqs = np.arange(T)[:, None] * (1.0 / 10000.0 ** (half / LOCAL_D))[None, :].astype(np.float32)
    freqs = np.concatenate([freqs, freqs], -1)
    base = (half + 0.4 * LOCAL_D) / (1.4 * LOCAL_D)
    power = (np.arange(T) - T // 2) / (WINDOW // 2)
    scale = base[None, :] ** power[:, None]
    scale = np.concatenate([scale, scale], -1)
    sign = np.where(np.arange(LOCAL_D) < LOCAL_D // 2, -1.0, 1.0)
    table = np.zeros((T, 2, 2, LOCAL_D))
    for m, s in enumerate((8.0 * scale, 1.0 / scale)):
        table[:, 0, m] = np.cos(freqs) * s
        table[:, 1, m] = np.roll(np.sin(freqs) * sign * s, LOCAL_D // 2, -1)
    return table.astype(np.float32)


def kernel(**inputs):
    import concourse.bacc as bacc
    from concourse.bass_utils import run_bass_kernel_spmd

    nc = bacc.Bacc("TRN2", target_bir_lowering=False, num_devices=1)
    arrays, args = {}, {}
    for name in _INS + ["rope"]:
        x = rope_table() if name == "rope" else np.ascontiguousarray(inputs[name])
        arrays[f"in_{name}_dram"] = x
        args[name] = nc.dram_tensor(f"in_{name}_dram", x.shape, mybir.dt.from_np(x.dtype), kind="ExternalInput").ap()
    out = nc.dram_tensor("out_0_dram", (SEQS, T, C), F32, kind="ExternalOutput").ap()
    macaron(nc, args, out)
    r = run_bass_kernel_spmd(nc, [arrays], core_ids=[0])
    return r.results[0]["out_0_dram"]
```
